# Optimizing a Trainium2 kernel written in Bass

```python
import numpy as np
import jax
import jax.numpy as jnp

def _softmax(x, axis=-1):
    return jax.nn.softmax(x, axis=axis)

def _gelu(x):
    return jax.nn.gelu(x, approximate=True)

def _silu(x):
    return jax.nn.silu(x)

def _sigmoid(x):
    return jax.nn.sigmoid(x)

def _layernorm(x, axis=-1, eps=1e-05):
    m = jnp.mean(x, axis=axis, keepdims=True)
    v = jnp.var(x, axis=axis, keepdims=True)
    return (x - m) / jnp.sqrt(v + eps)

def _scatter_add(tgt, idx, src, axis=0):
    return tgt.at[idx].add(src)

def _segment_sum(src, seg, n):
    return jax.ops.segment_sum(src, seg, n)
kernel_name = 'mk_gnn_resnorm_d4_gnn_r8_2075d3'

def setup_inputs(seed: int=0):
    np.random.seed(seed)
    _w = jnp.asarray

    def _rec_inputs():
        import jax
        import jax.numpy as jnp
        _gk = jax.random.key(seed)
        x = -0.0005121 + 1.001 * jax.random.normal(jax.random.fold_in(_gk, 1), (12500, 32), jnp.float32)
        _s = jax.random.randint(jax.random.fold_in(_gk, 2), (100000,), 0, 12500, jnp.int32)
        _d = jax.random.randint(jax.random.fold_in(_gk, 3), (100000,), 0, 12500, jnp.int32)
        _loop = jnp.arange(12500, dtype=jnp.int32)
        src = jnp.concatenate([_s, _d, _loop])
        dst = jnp.concatenate([_d, _s, _loop])
        _o = jnp.argsort(dst, stable=True)
        src = src[_o]
        dst = dst[_o]
        edge_attr_32 = -0.00010739 + 0.99994 * jax.random.normal(jax.random.fold_in(_gk, 12), (212500, 32), jnp.float32)
        edge_weight = jax.random.uniform(jax.random.fold_in(_gk, 14), (212500,), jnp.float32, 0.0, 1)
        return (x, src, dst, edge_attr_32, edge_weight)
    x, src, dst, edge_attr_32, edge_weight = _rec_inputs()

    def _L0_gnn_setup():
        import jax, jax.numpy as jnp
        import numpy as np
        N_NODES = 12500
        N_EDGES = 200000
        F_IN = 32
        F_OUT = 32
        key = jax.random.key(seed)
        kx, kr, kc, kv, kw = jax.random.split(key, 5)
        x = jax.random.normal(kx, (N_NODES, F_IN), dtype=jnp.float32)
        rows = jnp.sort(jax.random.randint(kr, (N_EDGES,), 0, N_NODES, dtype=jnp.int64))
        cols = jax.random.randint(kc, (N_EDGES,), 0, N_NODES, dtype=jnp.int64)
        vals = jax.random.uniform(kv, (N_EDGES,), dtype=jnp.float32)
        weight = jax.random.normal(kw, (F_IN, F_OUT), dtype=jnp.float32) / np.sqrt(F_IN)
        return {'x': x, 'rows': rows, 'cols': cols, 'vals': vals, 'weight': weight}
    _L0_gnn_all = _L0_gnn_setup()
    _L0_gnn_in = {k: v for k, v in _L0_gnn_all.items() if k in ('weight',)}
    del _L0_gnn_all

    def _L1_gnn_setup():
        import jax, jax.numpy as jnp
        import numpy as np
        N_NODES = 6250
        N_EDGES = 100000
        C_IN = 32
        C_OUT = 32
        BN_EPS = 1e-05

        def batch_norm(h, gamma, beta):
            mean = jnp.mean(h, axis=0)
            var = jnp.mean((h - mean) ** 2, axis=0)
            return (h - mean) * jax.lax.rsqrt(var + BN_EPS) * gamma + beta
        key = jax.random.key(seed)
        ks = jax.random.split(key, 8)
        x = jax.random.normal(ks[0], (N_NODES, C_IN), dtype=jnp.float32)
        edge_index = jax.random.randint(ks[1], (2, N_EDGES), 0, N_NODES, dtype=jnp.int64)
        s1 = 1.0 / np.sqrt(2 * C_IN)
        s2 = 1.0 / np.sqrt(C_OUT)
        W1 = jax.random.uniform(ks[2], (2 * C_IN, C_OUT), jnp.float32, -s1, s1)
        b1 = jax.random.uniform(ks[3], (C_OUT,), jnp.float32, -s1, s1)
        W2 = jax.random.uniform(ks[4], (C_OUT, C_OUT), jnp.float32, -s2, s2)
        b2 = jax.random.uniform(ks[5], (C_OUT,), jnp.float32, -s2, s2)
        gamma1 = jnp.ones((C_OUT,), jnp.float32)
        beta1 = jnp.zeros((C_OUT,), jnp.float32)
        gamma2 = jnp.ones((C_OUT,), jnp.float32)
        beta2 = jnp.zeros((C_OUT,), jnp.float32)
        return {'x': x, 'W1': W1, 'b1': b1, 'gamma1': gamma1, 'beta1': beta1, 'W2': W2, 'b2': b2, 'gamma2': gamma2, 'beta2': beta2, 'edge_index': edge_index}
    _L1_gnn_all = _L1_gnn_setup()
    _L1_gnn_in = {k: v for k, v in _L1_gnn_all.items() if k in ('W1', 'b1', 'gamma1', 'beta1', 'W2', 'b2', 'gamma2', 'beta2')}
    del _L1_gnn_all

    def _L2_gnn_setup():
        import jax, jax.numpy as jnp
        import numpy as np
        N_NODES = 12500
        N_EDGES = 200000
        NUM_FEATURES = 32
        HIDDEN = 64

        def _gcn_conv(h, W, b, src, dst, norm, inv_deg, n_nodes):
            h = h @ W
            msg = h[src] * norm[:, None]
            agg = jax.ops.segment_sum(msg, dst, num_segments=n_nodes)
            agg = agg + h * inv_deg[:, None]
            return agg + b
        key = jax.random.key(seed)
        k_x, k_e, k_w1, k_b1, k_w2, k_b2 = jax.random.split(key, 6)
        X = jax.random.normal(k_x, (N_NODES, NUM_FEATURES), dtype=jnp.float32)
        connections = jax.random.randint(k_e, (2, N_EDGES), 0, N_NODES, dtype=jnp.int64)
        W1 = jax.random.normal(k_w1, (NUM_FEATURES, HIDDEN), dtype=jnp.float32) / np.sqrt(NUM_FEATURES)
        b1 = jnp.zeros((HIDDEN,), dtype=jnp.float32)
        W2 = jax.random.normal(k_w2, (HIDDEN, NUM_FEATURES), dtype=jnp.float32) / np.sqrt(HIDDEN)
        b2 = jnp.zeros((NUM_FEATURES,), dtype=jnp.float32)
        return {'X': X, 'connections': connections, 'W1': W1, 'b1': b1, 'W2': W2, 'b2': b2}
    _L2_gnn_all = _L2_gnn_setup()
    _L2_gnn_in = {k: v for k, v in _L2_gnn_all.items() if k in ('W1', 'b1', 'W2', 'b2')}
    del _L2_gnn_all

    def _L3_gnn_setup():
        import jax, jax.numpy as jnp
        import numpy as np
        N_NODES = 12500
        N_EDGES = 50000
        D = 32
        EH = 128
        STEPS = 6

        def _gru_cell(x, h, wih, whh, bih, bhh):
            gi = x @ wih.T + bih
            gh = h @ whh.T + bhh
            ir, iz, inn = jnp.split(gi, 3, axis=-1)
            hr, hz, hn = jnp.split(gh, 3, axis=-1)
            r = jax.nn.sigmoid(ir + hr)
            z = jax.nn.sigmoid(iz + hz)
            n = jnp.tanh(inn + r * hn)
            return (1.0 - z) * n + z * h
        key = jax.random.key(seed)
        ks = jax.random.split(key, 12)
        s = 0.05
        return {'n_feat': jax.random.normal(ks[0], (N_NODES, D), jnp.float32), 'e_feat': jax.random.normal(ks[1], (N_EDGES, D), jnp.float32), 'src': jax.random.randint(ks[2], (N_EDGES,), 0, N_NODES, jnp.int32), 'dst': jax.random.randint(ks[3], (N_EDGES,), 0, N_NODES, jnp.int32), 'lin0_w': jax.random.normal(ks[4], (D, D), jnp.float32) * s, 'lin0_b': jnp.zeros((D,), jnp.float32), 'en1_w': jax.random.normal(ks[5], (EH, D), jnp.float32) * s, 'en1_b': jnp.zeros((EH,), jnp.float32), 'en2_w': jax.random.normal(ks[6], (D * D, EH), jnp.float32) * s, 'en2_b': jnp.zeros((D * D,), jnp.float32), 'conv_bias': jnp.zeros((D,), jnp.float32), 'gru_wih': jax.random.normal(ks[7], (3 * D, D), jnp.float32) * s, 'gru_whh': jax.random.normal(ks[8], (3 * D, D), jnp.float32) * s, 'gru_bih': jnp.zeros((3 * D,), jnp.float32), 'gru_bhh': jnp.zeros((3 * D,), jnp.float32)}
    _L3_gnn_all = _L3_gnn_setup()
    _L3_gnn_in = {k: v for k, v in _L3_gnn_all.items() if k in ('lin0_w', 'lin0_b', 'en1_w', 'en1_b', 'en2_w', 'en2_b', 'conv_bias', 'gru_wih', 'gru_whh', 'gru_bih', 'gru_bhh')}
    del _L3_gnn_all
    return {'x': x, 'src': src, 'dst': dst, 'edge_attr_32': edge_attr_32, 'edge_weight': edge_weight, 'L0_gnn_weight': _L0_gnn_in['weight'], 'L1_gnn_W1': _L1_gnn_in['W1'], 'L1_gnn_b1': _L1_gnn_in['b1'], 'L1_gnn_gamma1': _L1_gnn_in['gamma1'], 'L1_gnn_beta1': _L1_gnn_in['beta1'], 'L1_gnn_W2': _L1_gnn_in['W2'], 'L1_gnn_b2': _L1_gnn_in['b2'], 'L1_gnn_gamma2': _L1_gnn_in['gamma2'], 'L1_gnn_beta2': _L1_gnn_in['beta2'], 'L2_gnn_W1': _L2_gnn_in['W1'], 'L2_gnn_b1': _L2_gnn_in['b1'], 'L2_gnn_W2': _L2_gnn_in['W2'], 'L2_gnn_b2': _L2_gnn_in['b2'], 'L3_gnn_lin0_w': _L3_gnn_in['lin0_w'], 'L3_gnn_lin0_b': _L3_gnn_in['lin0_b'], 'L3_gnn_en1_w': _L3_gnn_in['en1_w'], 'L3_gnn_en1_b': _L3_gnn_in['en1_b'], 'L3_gnn_en2_w': _L3_gnn_in['en2_w'], 'L3_gnn_en2_b': _L3_gnn_in['en2_b'], 'L3_gnn_conv_bias': _L3_gnn_in['conv_bias'], 'L3_gnn_gru_wih': _L3_gnn_in['gru_wih'], 'L3_gnn_gru_whh': _L3_gnn_in['gru_whh'], 'L3_gnn_gru_bih': _L3_gnn_in['gru_bih'], 'L3_gnn_gru_bhh': _L3_gnn_in['gru_bhh']}

def reference(x, src, dst, edge_attr_32, edge_weight, L0_gnn_weight, L1_gnn_W1, L1_gnn_b1, L1_gnn_gamma1, L1_gnn_beta1, L1_gnn_W2, L1_gnn_b2, L1_gnn_gamma2, L1_gnn_beta2, L2_gnn_W1, L2_gnn_b1, L2_gnn_W2, L2_gnn_b2, L3_gnn_lin0_w, L3_gnn_lin0_b, L3_gnn_en1_w, L3_gnn_en1_b, L3_gnn_en2_w, L3_gnn_en2_b, L3_gnn_conv_bias, L3_gnn_gru_wih, L3_gnn_gru_whh, L3_gnn_gru_bih, L3_gnn_gru_bhh):
    import jax
    import jax.numpy as jnp

    def _L0_gnn_ref(x, rows, cols, vals, weight):
        import jax, jax.numpy as jnp
        import numpy as np
        N_NODES = 12500
        N_EDGES = 200000
        F_IN = 32
        F_OUT = 32
        gathered = x[cols] * vals[:, None]
        z = jax.ops.segment_sum(gathered, rows, num_segments=x.shape[0])
        return z @ weight

    def _L1_gnn_ref(x, W1, b1, gamma1, beta1, W2, b2, gamma2, beta2, edge_index):
        import jax, jax.numpy as jnp
        import numpy as np
        N_NODES = 6250
        N_EDGES = 100000
        C_IN = 32
        C_OUT = 32
        BN_EPS = 1e-05

        def batch_norm(h, gamma, beta):
            mean = jnp.mean(h, axis=0)
            var = jnp.mean((h - mean) ** 2, axis=0)
            return (h - mean) * jax.lax.rsqrt(var + BN_EPS) * gamma + beta
        row, col = (edge_index[0], edge_index[1])
        ef = jnp.concatenate([x[row], x[col]], axis=-1)
        h = jax.nn.relu(batch_norm(ef @ W1 + b1, gamma1, beta1))
        h = jax.nn.relu(batch_norm(h @ W2 + b2, gamma2, beta2))
        out = jax.ops.segment_sum(h, row, num_segments=x.shape[0])
        return out

    def _L2_gnn_ref(X, connections, W1, b1, W2, b2):
        import jax, jax.numpy as jnp
        import numpy as np
        N_NODES = 12500
        N_EDGES = 200000
        NUM_FEATURES = 32
        HIDDEN = 64

        def _gcn_conv(h, W, b, src, dst, norm, inv_deg, n_nodes):
            h = h @ W
            msg = h[src] * norm[:, None]
            agg = jax.ops.segment_sum(msg, dst, num_segments=n_nodes)
            agg = agg + h * inv_deg[:, None]
            return agg + b
        n_nodes = X.shape[0]
        src, dst = (connections[0], connections[1])
        ones = jnp.ones(src.shape[0], dtype=X.dtype)
        deg = jax.ops.segment_sum(ones, dst, num_segments=n_nodes) + 1.0
        inv_sqrt = jax.lax.rsqrt(deg)
        norm = inv_sqrt[src] * inv_sqrt[dst]
        inv_deg = 1.0 / deg
        h = _gcn_conv(X, W1, b1, src, dst, norm, inv_deg, n_nodes)
        h = _gcn_conv(h, W2, b2, src, dst, norm, inv_deg, n_nodes)
        return jax.nn.relu(h)

    def _L3_gnn_ref(n_feat, e_feat, src, dst, lin0_w, lin0_b, en1_w, en1_b, en2_w, en2_b, conv_bias, gru_wih, gru_whh, gru_bih, gru_bhh):
        import jax, jax.numpy as jnp
        import numpy as np
        N_NODES = 12500
        N_EDGES = 50000
        D = 32
        EH = 128
        STEPS = 6

        def _gru_cell(x, h, wih, whh, bih, bhh):
            gi = x @ wih.T + bih
            gh = h @ whh.T + bhh
            ir, iz, inn = jnp.split(gi, 3, axis=-1)
            hr, hz, hn = jnp.split(gh, 3, axis=-1)
            r = jax.nn.sigmoid(ir + hr)
            z = jax.nn.sigmoid(iz + hz)
            n = jnp.tanh(inn + r * hn)
            return (1.0 - z) * n + z * h
        n_nodes = n_feat.shape[0]
        out = jax.nn.relu(n_feat @ lin0_w.T + lin0_b)
        h = out
        eh = jax.nn.relu(e_feat @ en1_w.T + en1_b)
        w_e = (eh @ en2_w.T + en2_b).reshape(-1, D, D)
        for _ in range(STEPS):
            msg = jnp.einsum('ei,eio->eo', out[src], w_e)
            agg = jax.ops.segment_sum(msg, dst, num_segments=n_nodes) + conv_bias
            m = jax.nn.relu(agg)
            h = _gru_cell(m, h, gru_wih, gru_whh, gru_bih, gru_bhh)
            out = h
        return out
    edge_index = jnp.stack([src, dst])
    x = _layernorm(x + _L0_gnn_ref(x, src, dst, edge_weight, L0_gnn_weight), axis=-1)
    x = _layernorm(x + _L1_gnn_ref(x, L1_gnn_W1, L1_gnn_b1, L1_gnn_gamma1, L1_gnn_beta1, L1_gnn_W2, L1_gnn_b2, L1_gnn_gamma2, L1_gnn_beta2, edge_index), axis=-1)
    x = _layernorm(x + _L2_gnn_ref(x, edge_index, L2_gnn_W1, L2_gnn_b1, L2_gnn_W2, L2_gnn_b2), axis=-1)
    x = _layernorm(x + _L3_gnn_ref(x, edge_attr_32, src, dst, L3_gnn_lin0_w, L3_gnn_lin0_b, L3_gnn_en1_w, L3_gnn_en1_b, L3_gnn_en2_w, L3_gnn_en2_b, L3_gnn_conv_bias, L3_gnn_gru_wih, L3_gnn_gru_whh, L3_gnn_gru_bih, L3_gnn_gru_bhh), axis=-1)
    return x

_drawn_inputs = setup_inputs


def setup_inputs(seed=0):
    import zlib

    import numpy as np

    out = dict(_drawn_inputs(seed))
    spreads = {'L1_gnn_gamma1': (1.0, 0.2),
     'L1_gnn_beta1': (0.0, 0.1),
     'L1_gnn_gamma2': (1.0, 0.2),
     'L1_gnn_beta2': (0.0, 0.1),
     'L2_gnn_b1': (0.0, 0.1),
     'L2_gnn_b2': (0.0, 0.1),
     'L3_gnn_lin0_b': (0.0, 0.1),
     'L3_gnn_en1_b': (0.0, 0.1),
     'L3_gnn_en2_b': (0.0, 0.1),
     'L3_gnn_conv_bias': (0.0, 0.1),
     'L3_gnn_gru_bih': (0.0, 0.1),
     'L3_gnn_gru_bhh': (0.0, 0.1)}
    factors = {}
    for name, (base, spread) in spreads.items():
        noise = np.random.default_rng([zlib.crc32(name.encode()), seed]).standard_normal(out[name].shape)
        drawn = base * np.exp(spread * noise) if base else spread * noise
        out[name] = jnp.asarray(drawn.astype(out[name].dtype))
    for name, factor in factors.items():
        out[name] = (out[name] * factor).astype(out[name].dtype)
    return out
```

```python
from contextlib import ExitStack

import numpy as np

import concourse.bass as bass
from concourse import mybir

ALU = mybir.AluOpType
ACT = mybir.ActivationFunctionType
AX = mybir.AxisListType.X
F32 = mybir.dt.float32
BF16 = mybir.dt.bfloat16
I32 = mybir.dt.int32

P = 128
N = 12500
D = 32
E = 212500
NB = 100
LO = N // NB
CHUNK = 4096
CC = CHUNK // P
NCH = -(-E // CHUNK)
EP = NCH * CHUNK
COLS = EP // P
G = 16
NG = -(-((E + NB * (P - 1)) // P) // G)
NG += NG % 2
TILES = NG * G
SPARE = (EP - E + P - 1) // P
TT = TILES + SPARE
SR = 4
DR = 2 + D
EH = 128
HID = 64
STEPS = 6
EPS = 1e-5
W = NB * D
Q = NB // 4
GD = G * D


def build(nc, a, out):
    top = ExitStack()

    def dram(name, shape, dt=F32):
        return nc.dram_tensor(name, shape, dt).ap()

    class Phase(ExitStack):

        def __init__(self, tag):
            super().__init__()
            self.tag, self.sems = tag, []

        def sb(self, name, shape, dt=F32):
            return self.enter_context(nc.sbuf_tensor(f"{self.tag}_{name}", shape, dt))

        def ps(self, name, shape, dt=F32):
            return self.enter_context(nc.psum_tensor(f"{self.tag}_{name}", shape, dt))

        def sem(self, name):
            s = self.enter_context(nc.semaphore(f"{self.tag}_{name}"))
            self.sems.append(s)
            return s

        def end(self):
            with nc.Block() as block:
                @block.gpsimd
                def _(pool):
                    for s in self.sems:
                        pool.dma_reset(range(s.num, s.num + 1))
                        pool.sem_clear(s)

    src_bucket = dram("src_bucket", [EP], BF16)
    dst_bucket = dram("dst_bucket", [EP], BF16)
    src_lo = dram("src_lo", [EP])
    dst_lo = dram("dst_lo", [EP])
    by_src = dram("by_src", [P, TT, SR])
    by_dst = dram("by_dst", [P, TT, DR])
    dst_meta = dram("dst_meta", [P, TILES, 2])
    hid_t = dram("hid_t", [P, TILES * P])
    edge_h1 = dram("edge_h1", [P, TILES * D])
    edge_h2 = dram("edge_h2", [P, TILES * D])
    table = dram("table", [N + 1, D])
    wide_table = dram("wide_table", [N + 1, 2 * D])

    def nodes(t):
        return t[0:N, :].rearrange("(l b) f -> l b f", b=NB)

    with top:
        def sb(name, shape, dt=F32):
            return top.enter_context(nc.sbuf_tensor(name, shape, dt))

        ident = sb("ident", [P, P])
        ones = sb("ones", [P, P])
        ones_b = sb("ones_b", [P, 1], BF16)
        iota_lo = sb("iota_lo", [P, LO])
        iota_b16 = sb("iota_b16", [P, P], BF16)
        iota_p = sb("iota_p", [P, 1])
        before = sb("before", [P, P])
        same_f = sb("same_f", [P, P])
        eps_t = sb("eps_t", [P, 1])
        X = sb("X", [LO, W])
        ACC = sb("ACC", [LO, W])
        deg = sb("deg", [LO, NB])
        start_s = sb("start_s", [P, 1])
        start_d = sb("start_d", [P, 1])
        off_s = sb("off_s", [1, TILES], I32)
        off_d = sb("off_d", [1, TILES], I32)

        with Phase('const') as ph:
            ramp = ph.sb("ramp", [P, P])
            filled, made, done = ph.sem("filled"), ph.sem("made"), ph.sem("done")
            x_in = ph.sem("x_in")
            with nc.Block() as block:
                @block.sync
                def _(sp):
                    sp.dma_start(X[:, :], nodes(a["x"]).rearrange("l b f -> l (b f)")).then_inc(x_in, 16)
                    sp.dma_start(table[:, :], a["x"][:, :]).then_inc(x_in, 16)
                    sp.dma_start(wide_table[N:N + 1, :],
                                 a["zeros"][0:1, 0:2 * D]).then_inc(x_in, 16)
                    sp.wait_ge(x_in, 48)
                    sp.wait_ge(made, 4)
                    for i in range(4):
                        for j in range(4):
                            sp.dma_start(same_f[i * D:(i + 1) * D, j * D:(j + 1) * D],
                                         ident[0:D, 0:D]).then_inc(done, 16)
                    sp.wait_ge(done, 16 * 16)

                @block.gpsimd
                def _(pool):
                    pool.memset(ident[:, :], 0.0).then_inc(filled, 1)
                    pool.memset(before[:, :], 0.0).then_inc(filled, 1)
                    pool.wait_ge(filled, 2)
                    pool.affine_select(out=ident[:, :], in_=ident[:, :], compare_op=ALU.not_equal, fill=1.0,
                                       base=0, pattern=[[-1, P]], channel_multiplier=1).then_inc(made, 1)
                    pool.affine_select(out=before[:, :], in_=before[:, :], compare_op=ALU.is_ge, fill=1.0,
                                       base=0, pattern=[[-1, P]], channel_multiplier=1).then_inc(made, 1)
                    pool.iota(ramp[:, :], [[1, P]], base=0, channel_multiplier=0,
                              allow_small_or_imprecise_dtypes=True).then_inc(made, 1)
                    pool.iota(iota_p[:, :], [[0, 1]], base=0, channel_multiplier=1,
                              allow_small_or_imprecise_dtypes=True).then_inc(made, 1)

                @block.vector
                def _(dve):
                    dve.memset(ones[:, :], 1.0)
                    dve.memset(ones_b[:, :], 1.0)
                    dve.memset(eps_t[:, :], EPS)
                    dve.memset(ACC[:, :], 0.0)
                    dve.memset(deg[:, :], 0.0)
                    dve.wait_ge(made, 4)
                    dve.tensor_copy(iota_lo[:, :], ramp[:, 0:LO])
                    dve.tensor_copy(iota_b16[:, :], ramp[:, :])
                    dve.memset(before[:, NB:P], 0.0)
            ph.end()

        with Phase('keys') as ph:
            node = [ph.sb(f"node{k}", [P, COLS], I32) for k in range(2)]
            nf = ph.sb("nf", [P, COLS])
            qi = ph.sb("qi", [P, COLS], I32)
            fix = ph.sb("fix", [P, COLS])
            lo = [ph.sb(f"lo{k}", [P, COLS]) for k in range(2)]
            bucket = [ph.sb(f"bucket{k}", [P, COLS]) for k in range(2)]
            lo16 = [ph.sb(f"lo16{k}", [P, COLS], BF16) for k in range(2)]
            bucket16 = [ph.sb(f"bucket16{k}", [P, COLS], BF16) for k in range(2)]
            loaded, keyed, kept = ph.sem("loaded"), ph.sem("keyed"), ph.sem("kept")
            with nc.Block() as block:
                @block.sync
                def _(sp):
                    for k, name in enumerate(("src", "dst")):
                        sp.dma_start(node[k][:, :], a[name].rearrange("(p c) -> p c", p=P)).then_inc(loaded, 16)
                    for k, (bd, ld) in enumerate(((src_bucket, src_lo), (dst_bucket, dst_lo))):
                        sp.wait_ge(keyed, k + 1)
                        sp.dma_start(bd.rearrange("(p c) -> p c", p=P), bucket16[k][:, :]).then_inc(kept, 16)
                        sp.dma_start(ld.rearrange("(p c) -> p c", p=P), lo[k][:, :]).then_inc(kept, 16)
                    sp.wait_ge(kept, 64)

                @block.vector
                def _(dve):
                    dve.wait_ge(loaded, 32)
                    for k in range(2):
                        dve.tensor_copy(nf[:, :], node[k][:, :])
                        dve.drain()
                        dve.tensor_scalar(qi[:, :], nf[:, :], 1.0 / NB, None, ALU.mult)
                        dve.drain()
                        dve.tensor_copy(lo[k][:, :], qi[:, :])
                        dve.drain()
                        dve.scalar_tensor_tensor(out=bucket[k][:, :], in0=lo[k][:, :], scalar=-float(NB),
                                                 in1=nf[:, :], op0=ALU.mult, op1=ALU.add)
                        dve.drain()
                        dve.tensor_scalar(fix[:, :], bucket[k][:, :], 0.0, None, ALU.is_lt)
                        dve.drain()
                        dve.tensor_tensor(lo[k][:, :], lo[k][:, :], fix[:, :], ALU.subtract)
                        dve.drain()
                        dve.scalar_tensor_tensor(out=bucket[k][:, :], in0=fix[:, :], scalar=float(NB),
                                                 in1=bucket[k][:, :], op0=ALU.mult, op1=ALU.add)
                        dve.drain()
                        dve.tensor_scalar(fix[:, :], bucket[k][:, :], float(NB), None, ALU.is_ge)
                        dve.drain()
                        dve.tensor_tensor(lo[k][:, :], lo[k][:, :], fix[:, :], ALU.add)
                        dve.drain()
                        dve.scalar_tensor_tensor(out=bucket[k][:, :], in0=fix[:, :], scalar=-float(NB),
                                                 in1=bucket[k][:, :], op0=ALU.mult, op1=ALU.add)
                        dve.drain()
                        dve.tensor_scalar(fix[:, :], nf[:, :], float(N), float(NB), ALU.is_ge, ALU.mult)
                        dve.drain()
                        dve.tensor_tensor(bucket[k][:, :], bucket[k][:, :], fix[:, :], ALU.add)
                        dve.drain()
                        dve.tensor_copy(lo16[k][:, :], lo[k][:, :])
                        dve.drain()
                        dve.tensor_copy(bucket16[k][:, :], bucket[k][:, :]).then_inc(keyed, 1)
            ph.end()

            HG = 16
            HN = COLS // HG
            hit_lo = [ph.sb(f"hit_lo{s}", [P, HG, LO], BF16) for s in range(2)]
            hit_b = [[ph.sb(f"hit_b{k}{s}", [P, HG, NB], BF16) for s in range(2)] for k in range(2)]
            total = [ph.sb(f"total{k}", [NB, 1]) for k in range(2)]
            p_deg = [ph.ps(f"p_deg{s}", [P, 512]) for s in range(2)]
            p_tot = [ph.ps(f"p_tot{s}", [P, 512]) for s in range(2)]
            hits, counted, summed = ph.sem("hits"), ph.sem("counted"), ph.sem("summed")
            with nc.Block() as block:
                @block.vector
                def _(dve):
                    for k in range(2):
                        dve.memset(total[k][:, :], 0.0)
                    dve.drain().then_inc(summed, 2)

                    def add(n, s):
                        dve.wait_ge(counted, n + 1)
                        dve.wait_ge(summed, n + 2)
                        dve.tensor_tensor(deg[:, :], deg[:, :], p_deg[s][0:LO, 0:NB], ALU.add)
                        for k in range(2):
                            ins = dve.tensor_tensor(total[k][:, :], total[k][:, :], p_tot[s][0:NB, k:k + 1], ALU.add)
                        ins.then_inc(summed, 1)

                    def find(n, s):
                        cols = bass.ds(n * HG, HG)
                        wide = [P, HG, LO]
                        dve.tensor_tensor(hit_lo[s][:, :, :], iota_b16[:, None, 0:LO].broadcast_to(wide),
                                          lo16[1][:, cols][:, :, None].broadcast_to(wide), ALU.is_equal)
                        wide = [P, HG, NB]
                        for k in range(2):
                            ins = dve.tensor_tensor(hit_b[k][s][:, :, :], iota_b16[:, None, 0:NB].broadcast_to(wide),
                                                    bucket16[k][:, cols][:, :, None].broadcast_to(wide), ALU.is_equal)
                        ins.then_inc(hits, 1)

                    find(0, 0)
                    find(1, 1)
                    with dve.Fori(0, HN // 2 - 1) as i:
                        for s in range(2):
                            add(i * 2 + s, s)
                            find(i * 2 + (s + 2), s)
                    add(HN - 2, 0)
                    add(HN - 1, 1)

                @block.tensor
                def _(pe):
                    with pe.Fori(0, HN // 2) as i:
                        for s in range(2):
                            pe.wait_ge(hits, i * 2 + (s + 1))
                            pe.wait_ge(summed, i * 2 + (s + 1))
                            for t in range(HG):
                                first, last = t == 0, t == HG - 1
                                pe.matmul(p_deg[s][0:LO, 0:NB], hit_lo[s][:, t, :], hit_b[1][s][:, t, :],
                                          start=first, stop=last)
                            for k in range(2):
                                for t in range(HG):
                                    ins = pe.matmul(p_tot[s][0:NB, k:k + 1], hit_b[k][s][:, t, :], ones_b[:, :],
                                                    start=t == 0, stop=t == HG - 1)
                            ins.then_inc(counted, 1)
            ph.end()

            tiles_i = ph.sb("tiles_i", [NB, 2], I32)
            tiles_f = ph.sb("tiles_f", [NB, 2])
            spare = ph.sb("spare", [1, P])
            tile_no = ph.sb("tile_no", [P, TILES])
            begun = ph.sb("begun", [P, TILES])
            first_t = ph.sb("first_t", [P, 2])
            p_first = p_deg[0]
            p_row = [p_deg[1], p_tot[0], p_tot[1], ph.ps("p_row3", [P, 512])]
            RW = TILES // 4
            tiled, firsts, begun_s, rows_s, ramp_s = (ph.sem(n) for n in
                                                      ("tiled", "firsts", "begun_s", "rows_s", "ramp_s"))
            with nc.Block() as block:
                @block.gpsimd
                def _(pool):
                    pool.iota(tile_no[:, :], [[1, TILES]], base=0, channel_multiplier=0,
                              allow_small_or_imprecise_dtypes=True).then_inc(ramp_s, 1)

                @block.tensor
                def _(pe):
                    pe.wait_ge(tiled, 1)
                    pe.matmul(p_first[:, 0:2], before[0:NB, :], tiles_f[:, :], start=True, stop=False)
                    pe.matmul(p_first[:, 0:2], spare[:, :], ones[0:1, 0:2], start=False, stop=True).then_inc(firsts, 1)
                    for k in range(2):
                        pe.wait_ge(begun_s, 1 + 2 * k)
                        for c in range(4):
                            ins = pe.matmul(p_row[c][0:1, 0:RW], ones[0:NB, 0:1], begun[0:NB, c * RW:(c + 1) * RW],
                                            start=True, stop=True)
                        ins.then_inc(rows_s, 1)

                @block.vector
                def _(dve):
                    dve.memset(spare[:, :], 0.0)
                    dve.drain()
                    dve.memset(spare[:, NB:P], float(TILES))
                    for k in range(2):
                        dve.tensor_scalar(tiles_i[:, k:k + 1], total[k][:, :], float(P - 1), None, ALU.add)
                    dve.drain()
                    dve.tensor_scalar(tiles_i[:, :], tiles_i[:, :], 7, None, ALU.arith_shift_right)
                    dve.drain()
                    dve.tensor_copy(tiles_f[:, :], tiles_i[:, :]).then_inc(tiled, 1)
                    dve.wait_ge(firsts, 1)
                    dve.tensor_copy(first_t[:, :], p_first[:, 0:2])
                    dve.drain()
                    dve.tensor_scalar(start_s[:, :], first_t[:, 0:1], float(P), None, ALU.mult)
                    dve.tensor_scalar(start_d[:, :], first_t[:, 1:2], float(P), None, ALU.mult)
                    dve.wait_ge(ramp_s, 1)
                    for k, off in enumerate((off_s, off_d)):
                        dve.tensor_scalar(begun[:, :], tile_no[:, :], first_t[:, k:k + 1], None,
                                          ALU.is_ge).then_inc(begun_s, 1)
                        dve.wait_ge(rows_s, k + 1)
                        for c in range(4):
                            ins = dve.tensor_scalar(off[:, c * RW:(c + 1) * RW], p_row[c][0:1, 0:RW], -1.0, float(D),
                                                    ALU.add, ALU.mult)
                        ins.then_inc(begun_s, 1)
            ph.end()

        def order(other, bucket_d, lo_d, recs, R, start):
            FILLS = 28
            FILL = TT // FILLS
            K = NB + 1
            with Phase('order_' + other) as ph:
                bk = [ph.sb(f"bk{s}", [P, CHUNK], BF16) for s in range(2)]
                hit = ph.sb("hit", [P, CHUNK], BF16)
                count = ph.sb("count", [P, CHUNK])
                carry = ph.sb("carry", [P, 1])
                pos = ph.sb("pos", [P, CC], I32)
                row = ph.sb("row", [P, CC], I32)
                idx = [ph.sb(f"idx{s}", [P, CC], I32) for s in range(2)]
                rec = [ph.sb(f"rec{s}", [P, CC, R]) for s in range(2)]
                far = [ph.sb(f"far{s}", [P, CC], I32) for s in range(2)]
                lot = [ph.sb(f"lot{s}", [P, CC]) for s in range(2)]
                wgt = [ph.sb(f"wgt{s}", [P, CC]) for s in range(2)]
                empty = ph.sb("empty", [P, FILL, R])
                p_pos = ph.ps("p_pos", [P, 512])
                keys_in = [ph.sem(f"keys_in{s}") for s in range(2)]
                rec_in = [ph.sem(f"rec_in{s}") for s in range(2)]
                sent = [ph.sem(f"sent{s}") for s in range(2)]
                keys_free, placed, begun, ranked, indexed, packed, free, blank, filled = (
                    ph.sem(n) for n in ("keys_free", "placed", "begun", "ranked", "indexed", "packed", "free",
                                        "blank", "filled"))

                def chunk(ap, c):
                    return ap[bass.ds(c * CHUNK, CHUNK)]

                with nc.Block() as block:
                    @block.sync
                    def _(sp):
                        sp.wait_ge(blank, 1)
                        for f in range(FILLS):
                            sp.dma_start(recs[:, f * FILL:(f + 1) * FILL, :], empty[:, :, :]).then_inc(filled, 16)
                        with sp.Fori(0, NCH // 2) as i:
                            for s in range(2):
                                c = i * 2 + s
                                sp.wait_ge(keys_free, c + 1)
                                sp.sem_inc(begun, 1)
                                sp.dma_start(bk[s][0:K, :],
                                             chunk(bucket_d, c)[None, :].broadcast_to([K, CHUNK])).then_inc(keys_in[s], 16)
                                sp.wait_ge(free, c + 1)
                                sp.sem_inc(begun, 1)
                                for to, of in ((far[s], a[other]), (lot[s], lo_d)):
                                    sp.dma_start(to[:, :], chunk(of, c).rearrange("(p t) -> p t", t=CC)).then_inc(rec_in[s], 16)
                                if R == SR:
                                    of = chunk(a["edge_weight"], c).rearrange("(p t) -> p t", t=CC)
                                    sp.dma_start(wgt[s][:, :], of).then_inc(rec_in[s], 16)
                                else:
                                    of = a["edge_attr_32"][bass.ds(c * CHUNK, CHUNK), :].rearrange("(p t) f -> p t f", t=CC)
                                    sp.dma_start(rec[s][:, :, 2:R], of).then_inc(rec_in[s], 16)
                        sp.wait_ge(filled, 16 * FILLS)

                    @block.vector
                    def _(dve):
                        dve.memset(empty[:, :, :], 0.0)
                        dve.drain()
                        dve.memset(empty[:, :, 0:1].bitcast(I32), N)
                        dve.memset(empty[:, :, 1:2], -1.0).then_inc(blank, 1)
                        for s in range(2):
                            dve.memset(rec[s][:, :, :], 0.0)
                        dve.tensor_copy(carry[:, :], start[:, :]).then_inc(keys_free, 2)
                        with dve.Fori(0, NCH // 2) as i:
                            for s in range(2):
                                c = i * 2 + s
                                dve.wait_ge(keys_in[s], i * 16 + 16)
                                dve.tensor_scalar(hit[0:K, :], bk[s][0:K, :], iota_p[0:K, :], None,
                                                  ALU.is_equal).then_inc(keys_free, 1)
                                dve.drain()
                                dve.tensor_tensor_scan(count[0:K, :], hit[0:K, :], hit[0:K, :], carry[0:K, :],
                                                       ALU.add, ALU.max)
                                dve.drain()
                                dve.tensor_copy(carry[0:K, :], count[0:K, CHUNK - 1:CHUNK])
                                dve.drain()
                                dve.tensor_tensor(count[0:K, :], count[0:K, :], hit[0:K, :],
                                                  ALU.mult).then_inc(placed, 1)
                                dve.drain()
                                dve.wait_ge(ranked, c + 1)
                                dve.tensor_scalar(pos[:, :], p_pos[:, 0:CC], -1.0, None, ALU.add)
                                dve.drain()
                                dve.tensor_scalar(row[:, :], pos[:, :], P - 1, None, ALU.bitwise_and)
                                dve.tensor_scalar(pos[:, :], pos[:, :], 7, None, ALU.arith_shift_right)
                                dve.drain()
                                dve.wait_ge(free, c + 1)
                                dve.scalar_tensor_tensor(out=idx[s][:, :], in0=row[:, :], scalar=float(TT),
                                                         in1=pos[:, :], op0=ALU.mult, op1=ALU.add).then_inc(indexed, 1)

                    @block.tensor
                    def _(pe):
                        by_col = count[0:K, :].rearrange("k (p t) -> k t p", t=CC)
                        with pe.Fori(0, NCH) as c:
                            pe.wait_ge(placed, c + 1)
                            for t in range(CC):
                                ins = pe.matmul(p_pos[:, t:t + 1], by_col[:, t, :], ones[0:K, 0:1],
                                                start=True, stop=True)
                            ins.then_inc(ranked, 1)

                    @block.scalar
                    def _(act):
                        with act.Fori(0, NCH // 2) as i:
                            for s in range(2):
                                act.wait_ge(rec_in[s], i * 48 + 48)
                                ins = act.copy(rec[s][:, :, 0].bitcast(I32), far[s][:, :])
                                if R == SR:
                                    act.copy(rec[s][:, :, 2], wgt[s][:, :])
                                act.copy(rec[s][:, :, 1], lot[s][:, :]).then_inc(packed, 1)

                    @block.gpsimd
                    def _(pool):
                        rows = recs.rearrange("p t r -> (p t) r")

                        def send(i, s, first=False):
                            pool.wait_ge(indexed, i * 2 + (s + 1))
                            pool.wait_ge(packed, i * 2 + (s + 1))
                            pool.wait_ge(filled, 16 * FILLS)
                            pool.sem_inc(begun, 1)
                            for t in range(CC):
                                pool.indirect_dma_start(rows, bass.IndirectOffsetOnAxis(ap=idx[s][:, t:t + 1], axis=0),
                                                        rec[s][:, t, :], None).then_inc(sent[s], 16)
                            if not first:
                                pool.wait_ge(sent[1 - s], (i + s) * (16 * CC))
                                pool.sem_inc(free, 1)

                        pool.sem_inc(free, 2)
                        send(0, 0, first=True)
                        send(0, 1)
                        with pool.Fori(1, NCH // 2) as i:
                            send(i, 0)
                            send(i, 1)
                        pool.wait_ge(sent[1], NCH // 2 * 16 * CC)
                ph.end()

        order("src", dst_bucket, dst_lo, by_dst, DR, start_d)
        order("dst", src_bucket, src_lo, by_src, SR, start_s)
        TMP = sb("TMP", [LO, W])
        add_regs = [nc.vector.alloc_register(f"add_at{j}") for j in range(G)]
        row_regs = [nc.tensor.alloc_register(f"row_at{j}") for j in range(G)]

        def blocks(name, rows, cols, parts, of):
            t = sb(name, [rows * parts, cols * parts])
            weights.append((t, [(t[n * rows:(n + 1) * rows, n * cols:(n + 1) * cols], of) for n in range(parts)]))
            return t

        def column(name, parts, of):
            size = of.shape[0]
            t = sb(name, [size * parts, 1])
            weights.append((t, [(t[n * size:(n + 1) * size, :], of[:, None]) for n in range(parts)]))
            return t

        def across(name, of, rows=P):
            size = of.shape[0]
            t = sb(name, [rows, size])
            weights.append((t, [(t[:, :], of[None, :].broadcast_to([rows, size]))]))
            return t

        weights = []
        w0 = blocks("w0", D, D, 4, a["L0_gnn_weight"])
        w1a = blocks("w1a", D, D, 4, a["L1_gnn_W1"][0:D, :])
        w1b = blocks("w1b", D, D, 4, a["L1_gnn_W1"][D:2 * D, :])
        w12 = blocks("w12", D, D, 4, a["L1_gnn_W2"])
        b1c, g1c, be1c = (column(n, 4, a[f"L1_gnn_{n}"]) for n in ("b1", "gamma1", "beta1"))
        b2r, g2r, be2r = (across(n, a[f"L1_gnn_{n}"]) for n in ("b2", "gamma2", "beta2"))
        w21 = [sb(f"w21{h}", [P, P]) for h in range(2)]
        for h in range(2):
            weights.append((w21[h], [(w21[h][(2 * h + n) * D:(2 * h + n + 1) * D, n * HID:(n + 1) * HID], a["L2_gnn_W1"])
                                     for n in range(2)]))
        w22 = blocks("w22", HID, D, 2, a["L2_gnn_W2"])
        b21c = column("b21", 2, a["L2_gnn_b1"])
        b22r = across("b22", a["L2_gnn_b2"])
        lin0 = blocks("lin0", D, D, 4, a["lin0_t"])
        lin0b = across("lin0b", a["L3_gnn_lin0_b"])
        en1 = [sb(f"en1{n}", [P, EH]) for n in range(4)]
        for n in range(4):
            weights.append((en1[n], [(en1[n][n * D:(n + 1) * D, :], a["en1_t"])]))
        en1b = column("en1b", 1, a["L3_gnn_en1_b"])
        en2 = sb("en2", [EH, D * D])
        weights.append((en2, [(en2[:, :], a["en2_t"])]))
        en2b = blocks("en2b", D, D, 4, a["en2_b"])
        convb = column("convb", 4, a["L3_gnn_conv_bias"])
        wih = sb("wih", [P, 4 * P])
        whh = sb("whh", [P, 4 * P])
        gbias = sb("gbias", [1, 2 * 4 * P])
        for t, of, n3 in ((wih, a["wih_t"], 2), (whh, a["whh_t"], 3)):
            weights.append((t, [pair for n in range(4) for pair in (
                (t[n * D:(n + 1) * D, n * P:n * P + 2 * D], of[:, 0:2 * D]),
                (t[n * D:(n + 1) * D, n * P + n3 * D:n * P + (n3 + 1) * D], of[:, 2 * D:3 * D]))]))
        weights.append((gbias, [pair for n in range(4) for k, (of, n3) in enumerate(
            ((a["L3_gnn_gru_bih"], 2), (a["L3_gnn_gru_bhh"], 3))) for pair in (
                (gbias[:, (k * 4 + n) * P:(k * 4 + n) * P + 2 * D], of[None, 0:2 * D]),
                (gbias[:, (k * 4 + n) * P + n3 * D:(k * 4 + n) * P + (n3 + 1) * D], of[None, 2 * D:3 * D]))]))

        with Phase("weights") as ph:
            zeroed, w_in = ph.sem("zeroed"), ph.sem("w_in")
            with nc.Block() as block:
                @block.vector
                def _(dve):
                    for t, _ in weights:
                        dve.memset(t[:, :], 0.0).then_inc(zeroed, 1)

                @block.sync
                def _(sp):
                    n = 0
                    for k, (_, parts) in enumerate(weights):
                        sp.wait_ge(zeroed, k + 1)
                        for to, of in parts:
                            with nc.allow_non_contiguous_dma(reason="bias columns"):
                                sp.dma_start(to, of).then_inc(w_in, 16)
                            n += 1
                    sp.wait_ge(w_in, 16 * n)
            ph.end()

        def zero_row(width):
            return a["zeros"][0:1, 0:width]

        def f3(t):
            return t[:, :].rearrange("l (b f) -> l b f", f=D)

        def per_bucket(t):
            return t[:, :, None].broadcast_to([LO, NB, D])

        def layer_norm(tag, y, to):
            with Phase(tag) as ph:
                sq = ph.sb("sq", [LO, W])
                m, v = ph.sb("m", [LO, NB]), ph.sb("v", [LO, NB])
                centred, squared, varied, rooted = (ph.sem(n) for n in ("centred", "squared", "varied", "rooted"))
                with nc.Block() as block:
                    @block.vector
                    def _(dve):
                        dve.tensor_reduce(m[:, :], f3(y), AX, ALU.add)
                        dve.drain()
                        dve.tensor_scalar(m[:, :], m[:, :], 1.0 / D, None, ALU.mult)
                        dve.drain()
                        dve.tensor_tensor(f3(y), f3(y), per_bucket(m), ALU.subtract).then_inc(centred, 1)
                        dve.wait_ge(squared, 1)
                        dve.tensor_reduce(v[:, :], f3(sq), AX, ALU.add).then_inc(varied, 1)
                        dve.wait_ge(rooted, 1)
                        dve.reciprocal(v[:, :], v[:, :])
                        dve.drain()
                        dve.tensor_tensor(f3(to), f3(y), per_bucket(v), ALU.mult)

                    @block.scalar
                    def _(act):
                        act.wait_ge(centred, 1)
                        act.activation(sq[:, :], y[:, :], ACT.Square).then_inc(squared, 1)
                        act.wait_ge(varied, 1)
                        act.activation(v[:, :], v[:, :], ACT.Sqrt, bias=eps_t[0:LO, :],
                                       scale=1.0 / D).then_inc(rooted, 1)
                ph.end()

        def node_products(tag, source, rhs, take):
            with Phase(tag) as ph:
                turned = [ph.sb(f"turned{s}", [P, LO]) for s in range(2)]
                p_t = [ph.ps(f"p_t{s}", [P, 512]) for s in range(2)]
                p_o = [[ph.ps(f"p_o{s}{k}", [P, 512]) for k in range(len(rhs))] for s in range(2)]
                t_ok, c_ok, o_ok, taken = (ph.sem(n) for n in ("t_ok", "c_ok", "o_ok", "taken"))
                with nc.Block() as block:
                    @block.tensor
                    def _(pe):
                        def turn(q):
                            if q >= 2:
                                pe.wait_ge(c_ok, q - 1)
                            pe.transpose(p_t[q % 2][:, 0:LO], source[:, q * P:(q + 1) * P],
                                         ident[0:LO, 0:LO]).then_inc(t_ok, 1)

                        turn(0)
                        for q in range(Q):
                            if q + 1 < Q:
                                turn(q + 1)
                            pe.wait_ge(c_ok, q + 1)
                            if q >= 2:
                                pe.wait_ge(taken, q - 1)
                            for k, w in enumerate(rhs):
                                ins = pe.matmul(p_o[q % 2][k][0:LO, 0:P], turned[q % 2][:, :], w[:, :],
                                                start=True, stop=True)
                            ins.then_inc(o_ok, 1)

                    @block.scalar
                    def _(act):
                        for q in range(Q):
                            act.wait_ge(t_ok, q + 1)
                            if q >= 2:
                                act.wait_ge(o_ok, q - 1)
                            act.copy(turned[q % 2][:, :], p_t[q % 2][:, 0:LO]).then_inc(c_ok, 1)

                    @block.vector
                    def _(dve):
                        for q in range(Q):
                            dve.wait_ge(o_ok, q + 1)
                            take(dve, q, [p[0:LO, 0:P] for p in p_o[q % 2]]).then_inc(taken, 1)
                ph.end()

        def store_table(tag, parts):
            with Phase(tag) as ph:
                stored = ph.sem("stored")
                with nc.Block() as block:
                    @block.sync
                    def _(sp):
                        for to, of in parts:
                            sp.dma_start(to, of).then_inc(stored, 16)
                        sp.wait_ge(stored, 16 * len(parts))
                ph.end()

        def clear(t):
            with nc.Block() as block:
                @block.vector
                def _(dve):
                    dve.memset(t[:, :], 0.0)

        AHEAD = 2 * G

        def add_sums(dve, ph_added, summed, p_sum, off, acc, g, s):
            dve.load(add_regs, off[0:1, bass.ds(g * G, G)])
            dve.wait_ge(summed, g + 3)
            for j in range(G):
                at = dve.snap(add_regs[j], min_val=0, max_val=W - D)
                to = acc[0:LO, bass.ds(at, D)]
                dve.wait_ge(ph_added, g * G + (j + AHEAD))
                dve.tensor_tensor(to, to, p_sum[s][0:LO, j * D:(j + 1) * D], ALU.add).then_inc(ph_added, 1)

        def gather_sum(tag, meta, mr, tab, weighted, off, acc):
            with Phase(tag) as ph:
                mt = [ph.sb(f"mt{s}", [P, G, mr]) for s in range(2)]
                xg = [ph.sb(f"xg{s}", [P, G, D]) for s in range(2)]
                hit = [ph.sb(f"hit{s}", [P, G, LO]) for s in range(2)]
                p_sum = [ph.ps(f"p_sum{s}", [P, 512]) for s in range(2)]
                meta_in = [ph.sem(f"meta_in{s}") for s in range(2)]
                rows_in = [ph.sem(f"rows_in{s}") for s in range(2)]
                hits, summed, added, begun = (ph.sem(n) for n in ("hits", "summed", "added", "begun"))
                with nc.Block() as block:
                    @block.sync
                    def _(sp):
                        with sp.Fori(0, NG // 2) as i:
                            for s in range(2):
                                sp.wait_ge(summed, i * 2 + (s + 1))
                                sp.sem_inc(begun, 1)
                                sp.dma_start(mt[s][:, :, :], meta[:, bass.ds((i * 2 + s) * G, G), :]).then_inc(meta_in[s], 16)

                    @block.gpsimd
                    def _(pool):
                        with pool.Fori(0, NG // 2) as i:
                            for s in range(2):
                                pool.wait_ge(meta_in[s], i * 16 + 16)
                                pool.wait_ge(summed, i * 2 + (s + 1))
                                pool.sem_inc(begun, 1)
                                for j in range(G):
                                    pool.indirect_dma_start(
                                        xg[s][:, j, :], None, tab[:, :],
                                        bass.IndirectOffsetOnAxis(ap=mt[s][:, j, 0:1].bitcast(I32), axis=0)).then_inc(rows_in[s], 16)

                    @block.vector
                    def _(dve):
                        def find(i, s):
                            dve.wait_ge(meta_in[s], i * 16 + 16)
                            dve.wait_ge(summed, i * 2 + (s + 1))
                            for j in range(G):
                                if weighted:
                                    ins = dve.tensor_scalar(hit[s][:, j, :], iota_lo[:, :], mt[s][:, j, 1:2],
                                                            mt[s][:, j, 2:3], ALU.is_equal, ALU.mult)
                                else:
                                    ins = dve.tensor_scalar(hit[s][:, j, :], iota_lo[:, :], mt[s][:, j, 1:2],
                                                            None, ALU.is_equal)
                            ins.then_inc(hits, 1)

                        dve.sem_inc(added, AHEAD)
                        find(0, 0)
                        with dve.Fori(0, NG // 2 - 1) as i:
                            find(i, 1)
                            add_sums(dve, added, summed, p_sum, off, acc, i * 2, 0)
                            find(i + 1, 0)
                            add_sums(dve, added, summed, p_sum, off, acc, i * 2 + 1, 1)
                        find(NG // 2 - 1, 1)
                        add_sums(dve, added, summed, p_sum, off, acc, NG - 2, 0)
                        add_sums(dve, added, summed, p_sum, off, acc, NG - 1, 1)

                    @block.tensor
                    def _(pe):
                        pe.sem_inc(summed, 2)
                        with pe.Fori(0, NG // 2) as i:
                            for s in range(2):
                                pe.wait_ge(hits, i * 2 + (s + 1))
                                pe.wait_ge(rows_in[s], i * (16 * G) + 16 * G)
                                pe.wait_ge(added, (i * 2 + s) * G + G)
                                for j in range(G):
                                    ins = pe.matmul(p_sum[s][0:LO, j * D:(j + 1) * D], hit[s][:, j, :], xg[s][:, j, :],
                                                    start=True, stop=True)
                                ins.then_inc(summed, 1)
                ph.end()

        gather_sum("l0", by_src, SR, table, True, off_s, ACC)

        def plus_x(dve, q, p):
            cols = slice(q * P, (q + 1) * P)
            return dve.tensor_tensor(TMP[:, cols], X[:, cols], p[0], ALU.add)

        node_products("l0w", ACC, [w0], plus_x)
        layer_norm("l0n", TMP, X)
        def halves(dve, q, p):
            cols = slice(q * P, (q + 1) * P)
            dve.tensor_copy(TMP[:, cols], p[0])
            return dve.tensor_copy(ACC[:, cols], p[1])

        node_products("l1h", X, [w1a, w1b], halves)
        store_table("l1t", [(nodes(table), f3(ACC)), (table[N:N + 1, :], zero_row(D))])

        sums = sb("sums", [P, GD])
        squares = sb("squares", [P, GD])
        scale1, shift1 = sb("scale1", [P, 1]), sb("shift1", [P, 1])
        scale2, shift2 = sb("scale2", [P, D]), sb("shift2", [P, D])

        def tally(dve, v, sq, squared, n):
            dve.tensor_tensor(sums[:, :], sums[:, :], v, ALU.add)
            dve.wait_ge(squared, n)
            return dve.tensor_tensor(squares[:, :], squares[:, :], sq, ALU.add)

        with Phase("l1a") as ph:
            mt = [ph.sb(f"mt{s}", [P, G, SR]) for s in range(2)]
            xg = [ph.sb(f"xg{s}", [P, GD]) for s in range(2)]
            hit = [ph.sb(f"hit{s}", [P, G, LO]) for s in range(2)]
            hit_t = [ph.sb(f"hit_t{s}", [LO, 4 * P]) for s in range(2)]
            h = [ph.sb(f"h{s}", [P, GD]) for s in range(2)]
            sq = [ph.sb(f"sq{s}", [P, GD]) for s in range(2)]
            p_t = [ph.ps(f"p_t{s}", [P, 512]) for s in range(2)]
            p_h = [ph.ps(f"p_h{s}", [P, 512]) for s in range(2)]
            meta_in = [ph.sem(f"meta_in{s}") for s in range(2)]
            rows_in = [ph.sem(f"rows_in{s}") for s in range(2)]
            stored = [ph.sem(f"stored{s}") for s in range(2)]
            hits, turned, copied, near, ready, squared, tallied, begun, kept = (ph.sem(n) for n in (
                "hits", "turned", "copied", "near", "ready", "squared", "tallied", "begun", "kept"))
            with nc.Block() as block:
                @block.sync
                def _(sp):
                    def fetch(g, s):
                        sp.dma_start(mt[s][:, :, :], by_src[:, bass.ds(g * G, G), :]).then_inc(meta_in[s], 16)

                    sp.sem_inc(kept, 2)
                    with sp.Fori(0, NG // 2) as i:
                        for s in range(2):
                            sp.wait_ge(tallied, i * 2 + (s + 1))
                            sp.sem_inc(begun, 1)
                            fetch(i * 2 + s, s)

                @block.gpsimd
                def _(pool):
                    with pool.Fori(0, NG // 2) as i:
                        for s in range(2):
                            pool.wait_ge(meta_in[s], i * 16 + 16)
                            pool.wait_ge(tallied, i * 2 + (s + 1))
                            pool.sem_inc(begun, 1)
                            for j in range(G):
                                pool.indirect_dma_start(
                                    xg[s][:, j * D:(j + 1) * D], None, table[:, :],
                                    bass.IndirectOffsetOnAxis(ap=mt[s][:, j, 0:1].bitcast(I32), axis=0)).then_inc(rows_in[s], 16)

                @block.scalar
                def _(act):
                    def store(i, s):
                        act.dma_start(edge_h1[:, bass.ds((i * 2 + s) * GD, GD)], h[s][:, :]).then_inc(stored[s], 16)

                    act.sem_inc(copied, 2)
                    with act.Fori(0, NG // 2) as i:
                        for s in range(2):
                            for k in range(G // 4):
                                n = (i * 2 + s) * (G // 4) + k
                                act.wait_ge(turned, n + 1)
                                act.wait_ge(near, n + 1)
                                act.copy(hit_t[k % 2][:, :], p_t[k % 2][0:LO, :]).then_inc(copied, 1)
                            act.wait_ge(ready, i * 2 + (s + 1))
                            act.wait_ge(tallied, i * 2 + (s + 1))
                            act.activation(sq[s][:, :], h[s][:, :], ACT.Square).then_inc(squared, 1)
                            store(i, s)

                @block.tensor
                def _(pe):
                    pe.sem_inc(near, 2)
                    with pe.Fori(0, NG // 2) as i:
                        for s in range(2):
                            g = i * 2 + s
                            pe.load(row_regs, off_s[0:1, bass.ds(g * G, G)])
                            pe.wait_ge(hits, g + 1)
                            pe.wait_ge(tallied, g + 1)

                            def turn(k):
                                pe.wait_ge(copied, g * (G // 4) + (k + 1))
                                for t in range(4):
                                    ins = pe.transpose(p_t[k % 2][0:LO, t * P:(t + 1) * P], hit[s][:, 4 * k + t, :],
                                                       ident[:, :])
                                ins.then_inc(turned, 1)

                            turn(0)
                            for k in range(G // 4):
                                if k + 1 < G // 4:
                                    turn(k + 1)
                                pe.wait_ge(copied, g * (G // 4) + (k + 3))
                                for t in range(4):
                                    j = 4 * k + t
                                    at = pe.snap(row_regs[j], min_val=0, max_val=W - D)
                                    ins = pe.matmul(p_h[s][:, j * D:(j + 1) * D], hit_t[k % 2][:, t * P:(t + 1) * P],
                                                    TMP[0:LO, bass.ds(at, D)], start=True, stop=True)
                                ins.then_inc(near, 1)

                @block.vector
                def _(dve):
                    def find(i, s):
                        dve.wait_ge(meta_in[s], i * 16 + 16)
                        dve.wait_ge(tallied, i * 2 + (s + 1))
                        for j in range(G):
                            ins = dve.tensor_scalar(hit[s][:, j, :], iota_lo[:, :], mt[s][:, j, 1:2], None, ALU.is_equal)
                        ins.then_inc(hits, 1)

                    def join(i, s, again=True):
                        g = i * 2 + s
                        dve.wait_ge(near, g * (G // 4) + (G // 4 + 2))
                        dve.wait_ge(rows_in[s], i * (16 * G) + 16 * G)
                        if again:
                            dve.wait_ge(stored[s], i * 16)
                        dve.tensor_tensor(h[s][:, :], p_h[s][:, :], xg[s][:, :], ALU.add).then_inc(ready, 1)
                        dve.wait_ge(ready, g + 1)
                        dve.wait_ge(tallied, g + 2)
                        tally(dve, h[s][:, :], sq[s][:, :], squared, g + 1).then_inc(tallied, 1)

                    dve.memset(sums[:, :], 0.0)
                    dve.memset(squares[:, :], 0.0)
                    dve.drain().then_inc(tallied, 2)
                    find(0, 0)
                    find(0, 1)
                    join(0, 0, again=False)
                    find(1, 0)
                    join(0, 1, again=False)
                    with dve.Fori(1, NG // 2 - 1) as i:
                        find(i, 1)
                        join(i, 0)
                        find(i + 1, 0)
                        join(i, 1)
                    find(NG // 2 - 1, 1)
                    join(NG // 2 - 1, 0)
                    join(NG // 2 - 1, 1)
                    for s in range(2):
                        dve.wait_ge(stored[s], NG // 2 * 16)
            ph.end()

        def norm_terms(dve, s, q, g, be, b, mean, var, root, rooted, scale, shift, varied):
            dve.tensor_scalar(mean, s, 1.0 / E, None, ALU.mult)
            dve.tensor_scalar(var, q, 1.0 / E, None, ALU.mult)
            dve.drain()
            dve.tensor_tensor(shift, mean, mean, ALU.mult)
            dve.drain()
            dve.tensor_tensor(var, var, shift, ALU.subtract)
            dve.drain()
            dve.tensor_scalar(var, var, 0.0, None, ALU.max).then_inc(varied, 1)
            dve.wait_ge(rooted, 1)
            dve.reciprocal(var, root)
            dve.tensor_tensor(mean, mean, b, ALU.add)
            dve.drain()
            dve.tensor_tensor(scale, g, var, ALU.mult)
            dve.tensor_tensor(mean, b, mean, ALU.subtract)
            dve.drain()
            dve.tensor_tensor(shift, scale, mean, ALU.mult)
            dve.drain()
            dve.tensor_tensor(shift, shift, be, ALU.add)

        with Phase("l1s") as ph:
            cols = ph.sb("cols", [P, 2])
            mean, var, root, both = (ph.sb(n, [P, w]) for n, w in (("mean", 1), ("var", 1), ("root", 1), ("both", 2)))
            p_c = ph.ps("p_c", [P, 512])
            p_f = ph.ps("p_f", [P, 512])
            summed, cols_ok, folded, varied, rooted = (ph.sem(n) for n in ("summed", "cols_ok", "folded", "varied", "rooted"))
            with nc.Block() as block:
                @block.tensor
                def _(pe):
                    for k, t in enumerate((sums, squares)):
                        for c in range(4):
                            ins = pe.matmul(p_c[:, k:k + 1], t[:, c * P:(c + 1) * P], ones[:, 0:1],
                                            start=c == 0, stop=c == 3)
                    ins.then_inc(summed, 1)
                    pe.wait_ge(cols_ok, 1)
                    pe.matmul(p_f[:, 0:2], same_f[:, :], cols[:, :], start=True, stop=True).then_inc(folded, 1)

                @block.scalar
                def _(act):
                    act.wait_ge(varied, 1)
                    act.activation(root[:, :], var[:, :], ACT.Sqrt, bias=eps_t[:, :]).then_inc(rooted, 1)

                @block.vector
                def _(dve):
                    dve.wait_ge(summed, 1)
                    dve.tensor_copy(cols[:, :], p_c[:, 0:2]).then_inc(cols_ok, 1)
                    dve.wait_ge(folded, 1)
                    dve.tensor_copy(both[:, :], p_f[:, 0:2])
                    dve.drain()
                    norm_terms(dve, both[:, 0:1], both[:, 1:2], g1c[:, :], be1c[:, :], b1c[:, :], mean[:, :], var[:, :],
                               root[:, :], rooted, scale1[:, :], shift1[:, :], varied)
            ph.end()

        with Phase("l1b") as ph:
            mt = [ph.sb(f"mt{s}", [P, G, SR]) for s in range(2)]
            h = [ph.sb(f"h{s}", [P, GD]) for s in range(2)]
            act_t = [ph.sb(f"act_t{s}", [P, 4 * P]) for s in range(2)]
            real = [ph.sb(f"real{s}", [P, G]) for s in range(2)]
            h2 = [ph.sb(f"h2{s}", [P, GD]) for s in range(2)]
            sq = [ph.sb(f"sq{s}", [P, GD]) for s in range(2)]
            p_t = [ph.ps(f"p_t{s}", [P, 512]) for s in range(2)]
            p_h = [ph.ps(f"p_h{s}", [P, 512]) for s in range(2)]
            in_ = [ph.sem(f"in_{s}") for s in range(2)]
            stored = [ph.sem(f"stored{s}") for s in range(2)]
            turned, relued, mapped, ready, squared, tallied, begun = (ph.sem(n) for n in (
                "turned", "relued", "mapped", "ready", "squared", "tallied", "begun"))
            with nc.Block() as block:
                @block.sync
                def _(sp):
                    with sp.Fori(0, NG // 2) as i:
                        for s in range(2):
                            g = i * 2 + s
                            sp.wait_ge(tallied, g + 1)
                            sp.sem_inc(begun, 1)
                            sp.dma_start(h[s][:, :], edge_h1[:, bass.ds(g * GD, GD)]).then_inc(in_[s], 16)
                            sp.dma_start(mt[s][:, :, :], by_src[:, bass.ds(g * G, G), :]).then_inc(in_[s], 16)

                @block.tensor
                def _(pe):
                    def turn(i, s):
                        pe.wait_ge(in_[s], i * 32 + 32)
                        pe.wait_ge(relued, i * 2 + (s + 1))
                        for k in range(4):
                            ins = pe.transpose(p_t[s][:, k * P:(k + 1) * P], h[s][:, k * P:(k + 1) * P], ident[:, :])
                        ins.then_inc(turned, 1)

                    def times(i, s):
                        g = i * 2 + s
                        pe.wait_ge(relued, g + 3)
                        pe.wait_ge(tallied, g + 1)
                        for k in range(4):
                            ins = pe.matmul(p_h[s][:, k * P:(k + 1) * P], act_t[s][:, k * P:(k + 1) * P], w12[:, :],
                                            start=True, stop=True)
                        ins.then_inc(mapped, 1)

                    turn(0, 0)
                    with pe.Fori(0, NG // 2 - 1) as i:
                        turn(i, 1)
                        times(i, 0)
                        turn(i + 1, 0)
                        times(i, 1)
                    turn(NG // 2 - 1, 1)
                    times(NG // 2 - 1, 0)
                    times(NG // 2 - 1, 1)

                @block.scalar
                def _(act):
                    def relu(i, s):
                        act.wait_ge(turned, i * 2 + (s + 1))
                        act.wait_ge(tallied, i * 2 + (s + 1))
                        act.activation(act_t[s][:, :], p_t[s][:, :], ACT.Relu, bias=shift1[:, :],
                                       scale=scale1[:, :]).then_inc(relued, 1)

                    def square(i, s):
                        g = i * 2 + s
                        act.wait_ge(ready, g + 1)
                        act.wait_ge(tallied, g + 1)
                        act.activation(sq[s][:, :], h2[s][:, :], ACT.Square).then_inc(squared, 1)
                        act.dma_start(edge_h2[:, bass.ds(g * GD, GD)], h2[s][:, :]).then_inc(stored[s], 16)

                    act.sem_inc(relued, 2)
                    relu(0, 0)
                    with act.Fori(0, NG // 2 - 1) as i:
                        relu(i, 1)
                        square(i, 0)
                        relu(i + 1, 0)
                        square(i, 1)
                    relu(NG // 2 - 1, 1)
                    square(NG // 2 - 1, 0)
                    square(NG // 2 - 1, 1)

                @block.vector
                def _(dve):
                    def join(i, s, again=True):
                        g = i * 2 + s
                        dve.wait_ge(in_[s], i * 32 + 32)
                        dve.tensor_scalar(real[s][:, :], mt[s][:, :, 1], 0.0, None, ALU.is_ge)
                        dve.drain()
                        if again:
                            dve.wait_ge(stored[s], i * 16)
                        dve.wait_ge(mapped, g + 1)
                        dve.tensor_tensor(h2[s][:, :].rearrange("p (t f) -> p t f", f=D),
                                          p_h[s][:, :].rearrange("p (t f) -> p t f", f=D),
                                          real[s][:, :, None].broadcast_to([P, G, D]), ALU.mult).then_inc(ready, 1)
                        dve.wait_ge(ready, g + 1)
                        dve.wait_ge(tallied, g + 2)
                        tally(dve, h2[s][:, :], sq[s][:, :], squared, g + 1).then_inc(tallied, 1)

                    dve.memset(sums[:, :], 0.0)
                    dve.memset(squares[:, :], 0.0)
                    dve.memset(ACC[:, :], 0.0)
                    dve.drain().then_inc(tallied, 2)
                    join(0, 0, again=False)
                    join(0, 1, again=False)
                    with dve.Fori(1, NG // 2) as i:
                        join(i, 0)
                        join(i, 1)
                    for s in range(2):
                        dve.wait_ge(stored[s], NG // 2 * 16)
            ph.end()

        with Phase("l1u") as ph:
            mean, var, root = (ph.sb(n, [P, D]) for n in ("mean", "var", "root"))
            tot = [ph.sb(f"tot{k}", [P, D]) for k in range(2)]
            p_a = [ph.ps(f"p_a{k}", [P, 512]) for k in range(2)]
            summed, varied, rooted = (ph.sem(n) for n in ("summed", "varied", "rooted"))
            with nc.Block() as block:
                @block.tensor
                def _(pe):
                    for k, t in enumerate((sums, squares)):
                        ins = pe.matmul(p_a[k][:, :], ones[:, :], t[:, :], start=True, stop=True)
                    ins.then_inc(summed, 1)

                @block.scalar
                def _(act):
                    act.wait_ge(varied, 1)
                    act.activation(root[:, :], var[:, :], ACT.Sqrt, bias=eps_t[:, :]).then_inc(rooted, 1)

                @block.vector
                def _(dve):
                    dve.wait_ge(summed, 1)
                    for k in range(2):
                        dve.tensor_reduce(tot[k][:, :], p_a[k][:, :].rearrange("p (t f) -> p f t", f=D), AX, ALU.add)
                    dve.drain()
                    norm_terms(dve, tot[0][:, :], tot[1][:, :], g2r[:, :], be2r[:, :], b2r[:, :], mean[:, :], var[:, :],
                               root[:, :], rooted, scale2[:, :], shift2[:, :], varied)
            ph.end()

        with Phase("l1c") as ph:
            mt = [ph.sb(f"mt{s}", [P, G, SR]) for s in range(2)]
            h = [ph.sb(f"h{s}", [P, GD]) for s in range(2)]
            u = [ph.sb(f"u{s}", [P, GD]) for s in range(2)]
            hit = [ph.sb(f"hit{s}", [P, G, LO]) for s in range(2)]
            p_sum = [ph.ps(f"p_sum{s}", [P, 512]) for s in range(2)]
            in_ = [ph.sem(f"in_{s}") for s in range(2)]
            hits, moved, relued, summed, added, begun = (ph.sem(n) for n in ("hits", "moved", "relued", "summed", "added", "begun"))
            with nc.Block() as block:
                @block.sync
                def _(sp):
                    with sp.Fori(0, NG // 2) as i:
                        for s in range(2):
                            g = i * 2 + s
                            sp.wait_ge(summed, g + 1)
                            sp.sem_inc(begun, 1)
                            sp.dma_start(h[s][:, :], edge_h2[:, bass.ds(g * GD, GD)]).then_inc(in_[s], 16)
                            sp.dma_start(mt[s][:, :, :], by_src[:, bass.ds(g * G, G), :]).then_inc(in_[s], 16)

                @block.scalar
                def _(act):
                    with act.Fori(0, NG // 2) as i:
                        for s in range(2):
                            act.wait_ge(moved, i * 2 + (s + 1))
                            act.activation(u[s][:, :], u[s][:, :], ACT.Relu).then_inc(relued, 1)

                @block.vector
                def _(dve):
                    def find(i, s):
                        dve.wait_ge(in_[s], i * 32 + 32)
                        dve.wait_ge(summed, i * 2 + (s + 1))
                        v = u[s][:, :].rearrange("p (t f) -> p t f", f=D)
                        wide = [P, G, D]
                        dve.tensor_tensor(v, h[s][:, :].rearrange("p (t f) -> p t f", f=D),
                                          scale2[:, None, :].broadcast_to(wide), ALU.mult)
                        for j in range(G):
                            ins = dve.tensor_scalar(hit[s][:, j, :], iota_lo[:, :], mt[s][:, j, 1:2], None, ALU.is_equal)
                        ins.then_inc(hits, 1)
                        dve.drain()
                        dve.tensor_tensor(v, v, shift2[:, None, :].broadcast_to(wide), ALU.add).then_inc(moved, 1)

                    dve.sem_inc(added, AHEAD)
                    find(0, 0)
                    with dve.Fori(0, NG // 2 - 1) as i:
                        find(i, 1)
                        add_sums(dve, added, summed, p_sum, off_s, ACC, i * 2, 0)
                        find(i + 1, 0)
                        add_sums(dve, added, summed, p_sum, off_s, ACC, i * 2 + 1, 1)
                    find(NG // 2 - 1, 1)
                    add_sums(dve, added, summed, p_sum, off_s, ACC, NG - 2, 0)
                    add_sums(dve, added, summed, p_sum, off_s, ACC, NG - 1, 1)

                @block.tensor
                def _(pe):
                    pe.sem_inc(summed, 2)
                    with pe.Fori(0, NG // 2) as i:
                        for s in range(2):
                            pe.wait_ge(hits, i * 2 + (s + 1))
                            pe.wait_ge(relued, i * 2 + (s + 1))
                            pe.wait_ge(added, (i * 2 + s) * G + G)
                            for j in range(G):
                                ins = pe.matmul(p_sum[s][0:LO, j * D:(j + 1) * D], hit[s][:, j, :],
                                                u[s][:, j * D:(j + 1) * D], start=True, stop=True)
                            ins.then_inc(summed, 1)
            ph.end()

        def residual(tag, y):
            with nc.Block() as block:
                @block.vector
                def _(dve):
                    dve.tensor_tensor(TMP[:, :], X[:, :], y[:, :], ALU.add)
                    dve.drain()
                    dve.memset(ACC[:, :], 0.0)
            layer_norm(tag, TMP, X)

        residual("l1n", ACC)
        with Phase("edges") as ph:
            rec = [ph.sb(f"rec{s}", [P, G, DR]) for s in range(2)]
            head = [ph.sb(f"head{s}", [P, G, 2]) for s in range(2)]
            attr = [ph.sb(f"attr{s}", [P, GD]) for s in range(2)]
            attr_t = [ph.sb(f"attr_t{s}", [P, 4 * P]) for s in range(2)]
            hid = [ph.sb(f"hid{s}", [P, G * P]) for s in range(2)]
            p_t = [ph.ps(f"p_t{s}", [P, 512]) for s in range(2)]
            p_e = [ph.ps(f"p_e{n}", [P, 512]) for n in range(4)]
            rec_in = [ph.sem(f"rec_in{s}") for s in range(2)]
            kept = [ph.sem(f"kept{s}") for s in range(2)]
            parted, turned, copied, mapped, relued, begun = (ph.sem(n) for n in (
                "parted", "turned", "copied", "mapped", "relued", "begun"))
            with nc.Block() as block:
                @block.sync
                def _(sp):
                    with sp.Fori(0, NG // 2) as i:
                        for s in range(2):
                            g = i * 2 + s
                            sp.wait_ge(parted, g + 1)
                            sp.sem_inc(begun, 1)
                            sp.dma_start(rec[s][:, :, :], by_dst[:, bass.ds(g * G, G), :]).then_inc(rec_in[s], 16)

                @block.gpsimd
                def _(pool):
                    with pool.Fori(0, NG // 2) as i:
                        for s in range(2):
                            g = i * 2 + s
                            pool.wait_ge(relued, g * 4 + 8)
                            pool.sem_inc(begun, 1)
                            pool.dma_start(dst_meta[:, bass.ds(g * G, G), :], head[s][:, :, :]).then_inc(kept[s], 16)
                            pool.dma_start(hid_t[:, bass.ds(g * (G * P), G * P)], hid[s][:, :]).then_inc(kept[s], 16)
                    for s in range(2):
                        pool.wait_ge(kept[s], NG // 2 * 32)

                @block.vector
                def _(dve):
                    def part(i, s, again=True):
                        dve.wait_ge(rec_in[s], i * 16 + 16)
                        dve.wait_ge(copied, i * 2 + (s + 1))
                        if again:
                            dve.wait_ge(kept[s], i * 32)
                        dve.tensor_copy(attr[s][:, :].rearrange("p (t f) -> p t f", f=D), rec[s][:, :, 2:DR])
                        dve.tensor_copy(head[s][:, :, :], rec[s][:, :, 0:2]).then_inc(parted, 1)

                    dve.sem_inc(parted, 2)
                    part(0, 0, again=False)
                    part(0, 1, again=False)
                    with dve.Fori(1, NG // 2) as i:
                        part(i, 0)
                        part(i, 1)

                @block.tensor
                def _(pe):
                    def turn(i, s):
                        g = i * 2 + s
                        pe.wait_ge(parted, g + 3)
                        pe.wait_ge(copied, g + 1)
                        for k in range(4):
                            ins = pe.transpose(p_t[s][:, k * P:(k + 1) * P], attr[s][:, k * P:(k + 1) * P], ident[:, :])
                        ins.then_inc(turned, 1)

                    def times(i, s):
                        g = i * 2 + s
                        pe.wait_ge(copied, g + 3)
                        for n in range(4):
                            pe.wait_ge(relued, g * 4 + (n + 1))
                            pe.matmul(p_e[n][:, :], en1[n][:, :], attr_t[s][:, :], start=True, stop=True).then_inc(mapped, 1)

                    turn(0, 0)
                    with pe.Fori(0, NG // 2 - 1) as i:
                        turn(i, 1)
                        times(i, 0)
                        turn(i + 1, 0)
                        times(i, 1)
                    turn(NG // 2 - 1, 1)
                    times(NG // 2 - 1, 0)
                    times(NG // 2 - 1, 1)

                @block.scalar
                def _(act):
                    def copy(i, s):
                        g = i * 2 + s
                        act.wait_ge(turned, g + 1)
                        act.wait_ge(mapped, g * 4 + 1)
                        act.copy(attr_t[s][:, :], p_t[s][:, :]).then_inc(copied, 1)

                    def relu(i, s, again=True):
                        g = i * 2 + s
                        if again:
                            act.wait_ge(kept[s], i * 32)
                        to = hid[s][:, :].rearrange("p (k n e) -> p n k e", k=4, n=4)
                        for n in range(4):
                            act.wait_ge(mapped, g * 4 + (n + 9))
                            act.activation(to[:, n, :, :], p_e[n][:, :].rearrange("p (k e) -> p k e", k=4), ACT.Relu,
                                           bias=en1b[:, :]).then_inc(relued, 1)

                    act.sem_inc(copied, 2)
                    act.sem_inc(relued, 4)
                    act.sem_inc(mapped, 8)
                    copy(0, 0)
                    copy(0, 1)
                    relu(0, 0, again=False)
                    copy(1, 0)
                    relu(0, 1, again=False)
                    with act.Fori(1, NG // 2 - 1) as i:
                        copy(i, 1)
                        relu(i, 0)
                        copy(i + 1, 0)
                        relu(i, 1)
                    copy(NG // 2 - 1, 1)
                    relu(NG // 2 - 1, 0)
                    relu(NG // 2 - 1, 1)
            ph.end()

        inv_root, inv_deg = sb("inv_root", [LO, NB]), sb("inv_deg", [LO, NB])

        with Phase("l2d") as ph:
            root, one_more, rooted = ph.sb("root", [LO, NB]), ph.sem("one_more"), ph.sem("rooted")
            with nc.Block() as block:
                @block.vector
                def _(dve):
                    dve.tensor_scalar(deg[:, :], deg[:, :], 1.0, None, ALU.add).then_inc(one_more, 1)
                    dve.wait_ge(one_more, 1)
                    dve.reciprocal(inv_deg[:, :], deg[:, :])
                    dve.wait_ge(rooted, 1)
                    dve.reciprocal(inv_root[:, :], root[:, :])
                    dve.drain()
                    dve.tensor_tensor(f3(TMP), f3(X), per_bucket(inv_root), ALU.mult)

                @block.scalar
                def _(act):
                    act.wait_ge(one_more, 1)
                    act.activation(root[:, :], deg[:, :], ACT.Sqrt).then_inc(rooted, 1)
            ph.end()

        def gcn_sum(tag, v):
            with Phase(tag) as ph:
                own = ph.sb("own", [LO, W])
                with nc.Block() as block:
                    @block.vector
                    def _(dve):
                        dve.tensor_tensor(f3(ACC), f3(ACC), per_bucket(inv_root), ALU.mult)
                        dve.tensor_tensor(f3(own), f3(v), per_bucket(inv_deg), ALU.mult)
                        dve.drain()
                        dve.tensor_tensor(ACC[:, :], ACC[:, :], own[:, :], ALU.add)
                ph.end()

        store_table("l2t", [(nodes(table), f3(TMP))])
        gather_sum("l2a", dst_meta, 2, table, False, off_d, ACC)
        gcn_sum("l2e", X)

        V = sb("V", [LO, W])
        with Phase("l2w") as ph:
            turned = [ph.sb(f"turned{s}", [P, LO]) for s in range(2)]
            hid = [ph.sb(f"hid{s}", [P, 2 * LO]) for s in range(2)]
            p_t = [ph.ps(f"p_t{s}", [P, 512]) for s in range(2)]
            p_c = [ph.ps(f"p_c{s}", [P, 512]) for s in range(2)]
            p_o = [ph.ps(f"p_o{s}", [P, 512]) for s in range(2)]
            t_ok, c_ok, m_ok, h_ok, o_ok, taken = (ph.sem(n) for n in ("t_ok", "c_ok", "m_ok", "h_ok", "o_ok", "taken"))
            with nc.Block() as block:
                @block.tensor
                def _(pe):
                    for n in range(Q + 2):
                        if n < Q:
                            if n >= 2:
                                pe.wait_ge(c_ok, n - 1)
                            pe.transpose(p_t[n % 2][:, 0:LO], ACC[:, n * P:(n + 1) * P], ident[0:LO, 0:LO]).then_inc(t_ok, 1)
                        if 1 <= n <= Q:
                            q = n - 1
                            pe.wait_ge(c_ok, q + 1)
                            if q >= 2:
                                pe.wait_ge(h_ok, q - 1)
                            for k in range(2):
                                ins = pe.matmul(p_c[q % 2][:, k * LO:(k + 1) * LO], w21[k][:, :], turned[q % 2][:, :],
                                                start=True, stop=True)
                            ins.then_inc(m_ok, 1)
                        if n >= 2:
                            q = n - 2
                            pe.wait_ge(h_ok, q + 1)
                            if q >= 2:
                                pe.wait_ge(taken, q - 1)
                            for k in range(2):
                                ins = pe.matmul(p_o[q % 2][0:LO, k * 2 * D:(k + 1) * 2 * D],
                                                hid[q % 2][:, k * LO:(k + 1) * LO], w22[:, :], start=True, stop=True)
                            ins.then_inc(o_ok, 1)

                @block.scalar
                def _(act):
                    for n in range(Q + 1):
                        if n < Q:
                            act.wait_ge(t_ok, n + 1)
                            if n >= 2:
                                act.wait_ge(m_ok, n - 1)
                            act.copy(turned[n % 2][:, :], p_t[n % 2][:, 0:LO]).then_inc(c_ok, 1)
                        if n >= 1:
                            q = n - 1
                            act.wait_ge(m_ok, q + 1)
                            if q >= 2:
                                act.wait_ge(o_ok, q - 1)
                            act.activation(hid[q % 2][:, :], p_c[q % 2][:, 0:2 * LO], ACT.Identity,
                                           bias=b21c[:, :]).then_inc(h_ok, 1)

                @block.vector
                def _(dve):
                    for q in range(Q):
                        dve.wait_ge(o_ok, q + 1)
                        dve.tensor_copy(V[:, q * P:(q + 1) * P], p_o[q % 2][0:LO, 0:P]).then_inc(taken, 1)
                    dve.wait_ge(taken, Q)
                    dve.tensor_tensor(f3(TMP), f3(V), per_bucket(inv_root), ALU.mult)
                    dve.wait_ge(m_ok, Q)
                    dve.memset(ACC[:, :], 0.0)
            ph.end()

        store_table("l2u", [(nodes(table), f3(TMP))])
        gather_sum("l2b", dst_meta, 2, table, False, off_d, ACC)
        gcn_sum("l2f", V)
        with nc.Block() as block:
            @block.vector
            def _(dve):
                dve.tensor_tensor(f3(V), f3(ACC), b22r[0:LO, None, :].broadcast_to([LO, NB, D]), ALU.add)
                dve.drain()
                dve.tensor_scalar(V[:, :], V[:, :], 0.0, None, ALU.max)
        residual("l2n", V)
        STATE = sb("STATE", [LO, NB, 2 * D])
        state_t = sb("state_t", [P, Q * LO])

        def first_state(dve, q, p):
            return dve.tensor_tensor(f3(V)[:, 4 * q:4 * q + 4, :], p[0].rearrange("l (b f) -> l b f", f=D),
                                     lin0b[0:LO, None, :].broadcast_to([LO, 4, D]), ALU.add)

        node_products("l3i", X, [lin0], first_state)
        with nc.Block() as block:
            @block.vector
            def _(dve):
                dve.tensor_scalar(V[:, :], V[:, :], 0.0, None, ALU.max)

        class StateProducts:

            def __init__(self, ph):
                self.p_t = ph.ps("sp_t", [P, 512])
                self.p_b = ph.ps("sp_b", [P, 512])
                self.t_ok, self.c_ok, self.b_ok, self.taken = (ph.sem(n) for n in ("st_ok", "sc_ok", "sb_ok", "staken"))

            def turn(self, pe, q):
                if q >= 1:
                    pe.wait_ge(self.c_ok, q)
                pe.transpose(self.p_t[:, 0:LO], V[:, q * P:(q + 1) * P], ident[0:LO, 0:LO]).then_inc(self.t_ok, 1)

            def copy(self, act, q):
                act.wait_ge(self.t_ok, q + 1)
                act.copy(STATE[:, 4 * q:4 * q + 4, 0:D], f3(V)[:, 4 * q:4 * q + 4, :])
                act.copy(state_t[:, q * LO:(q + 1) * LO], self.p_t[:, 0:LO]).then_inc(self.c_ok, 1)

            def times(self, pe, q):
                pe.wait_ge(self.c_ok, q + 1)
                if q >= 1:
                    pe.wait_ge(self.taken, q)
                pe.matmul(self.p_b[0:LO, 0:P], state_t[:, q * LO:(q + 1) * LO], en2b[:, :],
                          start=True, stop=True).then_inc(self.b_ok, 1)

            def take(self, dve, q):
                dve.wait_ge(self.b_ok, q + 1)
                dve.tensor_copy(STATE[:, 4 * q:4 * q + 4, D:2 * D],
                                self.p_b[0:LO, 0:P].rearrange("l (b f) -> l b f", f=D)).then_inc(self.taken, 1)

        def store_state(tag):
            store_table(tag, [(wide_table[0:N, :].rearrange("(l b) f -> l b f", b=NB), STATE[:, :, :])])

        with Phase("l3s") as ph:
            products = StateProducts(ph)
            with nc.Block() as block:
                @block.tensor
                def _(pe):
                    products.turn(pe, 0)
                    for q in range(Q):
                        if q + 1 < Q:
                            products.turn(pe, q + 1)
                        products.times(pe, q)

                @block.scalar
                def _(act):
                    for q in range(Q):
                        products.copy(act, q)

                @block.vector
                def _(dve):
                    for q in range(Q):
                        products.take(dve, q)
            ph.end()
        store_state("l3t")

        with nc.Fori(0, STEPS) as step:
            with Phase("l3m") as ph:
                HD = D * D
                mt = [ph.sb(f"mt{s}", [P, G, 2]) for s in range(2)]
                hid = [ph.sb(f"hid{s}", [P, G * P]) for s in range(2)]
                xg = [ph.sb(f"xg{s}", [P, G, 2 * D]) for s in range(2)]
                apart = [ph.sb(f"apart{s}", [P, G, LO]) for s in range(2)]
                prod = [ph.sb(f"prod{s}", [P, HD]) for s in range(2)]
                msg = [ph.sb(f"msg{s}", [P, GD]) for s in range(2)]
                p_w = [ph.ps(f"p_w{s}", [P, HD]) for s in range(2)]
                p_sum = [ph.ps(f"p_sum{s}", [P, 512]) for s in range(2)]
                meta_in = [ph.sem(f"meta_in{s}") for s in range(2)]
                hid_in = [ph.sem(f"hid_in{s}") for s in range(2)]
                rows_in = [ph.sem(f"rows_in{s}") for s in range(2)]
                distances, hits, mats, used, msgs, summed, added, begun = (ph.sem(n) for n in (
                    "distances", "hits", "mats", "used", "msgs", "summed", "added", "begun"))
                LAG = 3
                with nc.Block() as block:
                    @block.sync
                    def _(sp):
                        with sp.Fori(0, NG // 2) as i:
                            for s in range(2):
                                g = i * 2 + s
                                sp.wait_ge(summed, g + 1)
                                sp.sem_inc(begun, 1)
                                sp.dma_start(mt[s][:, :, :], dst_meta[:, bass.ds(g * G, G), :]).then_inc(meta_in[s], 16)
                                sp.dma_start(hid[s][:, :], hid_t[:, bass.ds(g * (G * P), G * P)]).then_inc(hid_in[s], 16)

                    @block.gpsimd
                    def _(pool):
                        with pool.Fori(0, NG // 2) as i:
                            for s in range(2):
                                pool.wait_ge(meta_in[s], i * 16 + 16)
                                pool.wait_ge(summed, i * 2 + (s + 1))
                                pool.sem_inc(begun, 1)
                                for j in range(G):
                                    pool.indirect_dma_start(
                                        xg[s][:, j, :], None, wide_table[:, :],
                                        bass.IndirectOffsetOnAxis(ap=mt[s][:, j, 0:1].bitcast(I32), axis=0)).then_inc(rows_in[s], 16)

                    @block.scalar
                    def _(act):
                        with act.Fori(0, NG // 2) as i:
                            for s in range(2):
                                g = i * 2 + s
                                act.wait_ge(meta_in[s], i * 16 + 16)
                                act.wait_ge(summed, g + 1)
                                for j in range(G):
                                    ins = act.activation(apart[s][:, j, :], iota_lo[:, :], ACT.Abs, scale=-1.0,
                                                         bias=mt[s][:, j, 1:2])
                                ins.then_inc(distances, 1)
                                act.wait_ge(distances, g + 1)
                                act.activation(apart[s][:, :, :], apart[s][:, :, :], ACT.Relu, scale=-1.0,
                                               bias=ones[:, 0:1]).then_inc(hits, 1)

                    @block.tensor
                    def _(pe):
                        def matrices(i, s, j):
                            t = (i * 2 + s) * G + j
                            pe.wait_ge(used, t + 1)
                            for c in range(2):
                                ins = pe.matmul(p_w[j % 2][:, c * 512:(c + 1) * 512], hid[s][:, j * P:(j + 1) * P],
                                                en2[:, c * 512:(c + 1) * 512], start=True, stop=True)
                            ins.then_inc(mats, 1)

                        def sum_up(i, s, j):
                            g = i * 2 + s
                            if j == 0:
                                pe.wait_ge(hits, g + 1)
                                pe.wait_ge(rows_in[s], i * (16 * G) + 16 * G)
                                pe.wait_ge(added, g * G + G)
                            pe.wait_ge(msgs, g * G + (j + 1))
                            to = p_sum[s][0:LO, j * D:(j + 1) * D]
                            pe.matmul(to, apart[s][:, j, :], msg[s][:, j * D:(j + 1) * D], start=True, stop=False)
                            ins = pe.matmul(to, apart[s][:, j, :], xg[s][:, j, D:2 * D], start=False, stop=True)
                            if j == G - 1:
                                ins.then_inc(summed, 1)

                        def group(i, s, first=False):
                            pe.wait_ge(hid_in[s], i * 16 + 16)
                            for j in range(G):
                                matrices(i, s, j)
                                if j >= LAG:
                                    sum_up(i, s, j - LAG)
                                elif not first:
                                    sum_up(i + (s - 1), 1 - s, G - LAG + j)

                        pe.sem_inc(summed, 2)
                        group(0, 0, first=True)
                        group(0, 1)
                        with pe.Fori(1, NG // 2) as i:
                            group(i, 0)
                            group(i, 1)
                        for j in range(G - LAG, G):
                            sum_up(NG // 2 - 1, 1, j)

                    @block.vector
                    def _(dve):
                        def add(g, s, j):
                            at = dve.snap(add_regs[j], min_val=0, max_val=W - D)
                            to = ACC[0:LO, bass.ds(at, D)]
                            dve.wait_ge(added, g * G + (j + AHEAD))
                            dve.tensor_tensor(to, to, p_sum[s][0:LO, j * D:(j + 1) * D], ALU.add).then_inc(added, 1)

                        def reduce(g, s, j):
                            dve.wait_ge(used, g * G + (j + 3))
                            dve.tensor_reduce(msg[s][:, j * D:(j + 1) * D],
                                              prod[j % 2][:, :].rearrange("p (o i) -> p o i", i=D), AX,
                                              ALU.add).then_inc(msgs, 1)

                        def group(i, s, first=False, later=False):
                            g = i * 2 + s
                            if not first:
                                dve.load(add_regs, off_d[0:1, bass.ds((g - 1) * G, G)])
                            dve.wait_ge(rows_in[s], i * (16 * G) + 16 * G)
                            if later:
                                dve.wait_ge(summed, g + 1)
                            for j in range(G):
                                dve.wait_ge(mats, g * G + (j + 1))
                                if not first or j >= 2:
                                    dve.wait_ge(msgs, g * G + (j - 1))
                                dve.tensor_tensor(prod[j % 2][:, :].rearrange("p (o i) -> p o i", i=D),
                                                  p_w[j % 2][:, :].rearrange("p (o i) -> p o i", i=D),
                                                  xg[s][:, j, None, 0:D].broadcast_to([P, D, D]),
                                                  ALU.mult).then_inc(used, 1)
                                if not first and 6 <= j < 14:
                                    if j == 6:
                                        dve.wait_ge(summed, g + 2)
                                    add(g - 1, 1 - s, 2 * (j - 6))
                                    add(g - 1, 1 - s, 2 * (j - 6) + 1)
                                if j:
                                    reduce(g, s, j - 1)
                            reduce(g, s, G - 1)

                        dve.sem_inc(used, 2)
                        dve.sem_inc(added, AHEAD)
                        group(0, 0, first=True)
                        group(0, 1)
                        with dve.Fori(1, NG // 2) as i:
                            group(i, 0, later=True)
                            group(i, 1, later=True)
                        add_sums(dve, added, summed, p_sum, off_d, ACC, NG - 1, 1)
                ph.end()

            with Phase("l3g") as ph:
                products = StateProducts(ph)
                m_t = [ph.sb(f"m_t{s}", [P, LO]) for s in range(2)]
                gate = [ph.sb(f"gate{s}", [LO, 4, 2 * D]) for s in range(2)]
                new = [ph.sb(f"new{s}", [LO, 4, D]) for s in range(2)]
                diff = [ph.sb(f"diff{s}", [LO, 4, D]) for s in range(2)]
                p_t = [ph.ps(f"p_t{s}", [P, 512]) for s in range(2)]
                p_g = [ph.ps(f"p_g{s}", [P, 512]) for s in range(2)]
                t_ok, m_ok, g_ok, s_ok, n_in, n_ok, h_ok = (ph.sem(n) for n in (
                    "t_ok", "m_ok", "g_ok", "s_ok", "n_in", "n_ok", "h_ok"))

                def gates(q):
                    return p_g[q % 2][0:LO, :].rearrange("l (b c) -> l b c", b=4)

                with nc.Block() as block:
                    @block.tensor
                    def _(pe):
                        for n in range(Q + 4):
                            if n < Q:
                                if n >= 2:
                                    pe.wait_ge(m_ok, n - 1)
                                pe.transpose(p_t[n % 2][:, 0:LO], ACC[:, n * P:(n + 1) * P],
                                             ident[0:LO, 0:LO]).then_inc(t_ok, 1)
                            if 1 <= n <= Q:
                                q = n - 1
                                if q >= 2:
                                    pe.wait_ge(n_in, q - 1)
                                to = p_g[q % 2][0:LO, :]
                                for k in range(2):
                                    pe.matmul(to, ones[0:1, 0:LO], gbias[:, k * 4 * P:(k + 1) * 4 * P],
                                              start=k == 0, stop=False)
                                pe.matmul(to, state_t[:, q * LO:(q + 1) * LO], whh[:, :], start=False, stop=False)
                                pe.wait_ge(m_ok, q + 1)
                                pe.matmul(to, m_t[q % 2][:, :], wih[:, :], start=False, stop=True).then_inc(g_ok, 1)
                            if 3 <= n < Q + 3:
                                pe.wait_ge(h_ok, n - 2)
                                products.turn(pe, n - 3)
                            if n >= 4:
                                products.times(pe, n - 4)

                    @block.scalar
                    def _(act):
                        for n in range(Q + 3):
                            if n < Q:
                                act.wait_ge(t_ok, n + 1)
                                if n >= 2:
                                    act.wait_ge(g_ok, n - 1)
                                act.activation(m_t[n % 2][:, :], p_t[n % 2][:, 0:LO], ACT.Relu,
                                               bias=convb[:, :]).then_inc(m_ok, 1)
                            if 1 <= n <= Q:
                                q = n - 1
                                act.wait_ge(g_ok, q + 1)
                                if q >= 2:
                                    act.wait_ge(h_ok, q - 1)
                                act.activation(gate[q % 2][:, :, :], gates(q)[:, :, 0:2 * D], ACT.Sigmoid).then_inc(s_ok, 1)
                            if 2 <= n < Q + 2:
                                q = n - 2
                                act.wait_ge(n_in, q + 1)
                                act.activation(new[q % 2][:, :, :], new[q % 2][:, :, :], ACT.Tanh).then_inc(n_ok, 1)
                            if n >= 3:
                                products.copy(act, n - 3)

                    @block.vector
                    def _(dve):
                        for n in range(1, Q + 4):
                            if n <= Q:
                                q = n - 1
                                dve.wait_ge(s_ok, q + 1)
                                if q >= 2:
                                    dve.wait_ge(h_ok, q - 1)
                                c = new[q % 2][:, :, :]
                                dve.tensor_tensor(c, gate[q % 2][:, :, 0:D], gates(q)[:, :, 3 * D:4 * D], ALU.mult)
                                dve.drain()
                                dve.tensor_tensor(c, c, gates(q)[:, :, 2 * D:3 * D], ALU.add).then_inc(n_in, 1)
                            if 2 <= n < Q + 2:
                                q = n - 2
                                state = f3(V)[:, 4 * q:4 * q + 4, :]
                                d = diff[q % 2][:, :, :]
                                dve.wait_ge(n_ok, q + 1)
                                dve.tensor_tensor(d, state, new[q % 2][:, :, :], ALU.subtract)
                                dve.drain()
                                dve.tensor_tensor(d, d, gate[q % 2][:, :, D:2 * D], ALU.mult)
                                dve.drain()
                                dve.tensor_tensor(state, d, new[q % 2][:, :, :], ALU.add).then_inc(h_ok, 1)
                            if n >= 4:
                                products.take(dve, n - 4)
                        dve.wait_ge(t_ok, Q)
                        dve.memset(ACC[:, :], 0.0)
                ph.end()
            store_state("l3u")

        with nc.Block() as block:
            @block.vector
            def _(dve):
                dve.tensor_tensor(TMP[:, :], X[:, :], V[:, :], ALU.add)
        layer_norm("l3n", TMP, X)
        store_table("end", [(out.rearrange("(l b) f -> l (b f)", b=NB), X[:, :])])


def arranged(inputs):
    x = {k: np.asarray(v) for k, v in inputs.items()}
    pad = EP - E

    def t(name):
        return np.ascontiguousarray(x[name].T)

    arrays = {
        "x": np.concatenate([x["x"], np.zeros((1, D), np.float32)]),
        "zeros": np.zeros((1, 2 * D), np.float32),
        "src": np.concatenate([x["src"], np.full(pad, N, x["src"].dtype)]),
        "dst": np.concatenate([x["dst"], np.full(pad, N, x["dst"].dtype)]),
        "edge_weight": np.concatenate([x["edge_weight"], np.zeros(pad, np.float32)]),
        "edge_attr_32": np.concatenate([x["edge_attr_32"], np.zeros((pad, D), np.float32)]),
        "lin0_t": t("L3_gnn_lin0_w"),
        "en1_t": t("L3_gnn_en1_w"),
        "wih_t": t("L3_gnn_gru_wih"),
        "whh_t": t("L3_gnn_gru_whh"),
        "en2_t": np.ascontiguousarray(x["L3_gnn_en2_w"].reshape(D, D, EH).transpose(2, 1, 0).reshape(EH, D * D)),
        "en2_b": x["L3_gnn_en2_b"].reshape(D, D),
    }
    for name in ("L0_gnn_weight", "L1_gnn_W1", "L1_gnn_b1", "L1_gnn_gamma1", "L1_gnn_beta1", "L1_gnn_W2",
                 "L1_gnn_b2", "L1_gnn_gamma2", "L1_gnn_beta2", "L2_gnn_W1", "L2_gnn_b1", "L2_gnn_W2", "L2_gnn_b2",
                 "L3_gnn_lin0_b", "L3_gnn_en1_b", "L3_gnn_conv_bias", "L3_gnn_gru_bih", "L3_gnn_gru_bhh"):
        arrays[name] = x[name]
    return arrays


def kernel(**inputs):
    import concourse.bacc as bacc
    from concourse.bass_utils import run_bass_kernel_spmd

    nc = bacc.Bacc("TRN2", target_bir_lowering=False, num_devices=1)
    arrays, args = {}, {}
    for name, v in arranged(inputs).items():
        arrays[f"in_{name}"] = np.ascontiguousarray(v)
        args[name] = nc.dram_tensor(f"in_{name}", v.shape, mybir.dt.from_np(v.dtype), kind="ExternalInput").ap()
    out = nc.dram_tensor("out_x", (N, D), F32, kind="ExternalOutput").ap()
    build(nc, args, out)
    r = run_bass_kernel_spmd(nc, [arrays], core_ids=[0])
    return r.results[0]["out_x"]
```

```python
from contextlib import ExitStack

import numpy as np

import concourse.bass as bass
from concourse import mybir

ALU = mybir.AluOpType
ACT = mybir.ActivationFunctionType
AX = mybir.AxisListType.X
F32 = mybir.dt.float32
BF16 = mybir.dt.bfloat16
I32 = mybir.dt.int32

P = 128
N = 12500
D = 32
E = 212500
NB = 100
LO = N // NB
CHUNK = 4096
CC = CHUNK // P
NCH = -(-E // CHUNK)
EP = NCH * CHUNK
COLS = EP // P
G = 16
NG = -(-((E + NB * (P - 1)) // P) // G)
NG += NG % 2
TILES = NG * G
SPARE = (EP - E + P - 1) // P
TT = TILES + SPARE
SR = 4
DR = 2 + D
EH = 128
HID = 64
STEPS = 6
EPS = 1e-5
W = NB * D
Q = NB // 4
GD = G * D


def build(nc, a, out):
    top = ExitStack()

    def dram(name, shape, dt=F32):
        return nc.dram_tensor(name, shape, dt).ap()

    class Phase(ExitStack):

        def __init__(self, tag):
            super().__init__()
            self.tag, self.sems = tag, []

        def sb(self, name, shape, dt=F32):
            return self.enter_context(nc.sbuf_tensor(f"{self.tag}_{name}", shape, dt))

        def ps(self, name, shape, dt=F32):
            return self.enter_context(nc.psum_tensor(f"{self.tag}_{name}", shape, dt))

        def sem(self, name):
            s = self.enter_context(nc.semaphore(f"{self.tag}_{name}"))
            self.sems.append(s)
            return s

        def end(self):
            with nc.Block() as block:
                @block.gpsimd
                def _(pool):
                    for s in self.sems:
                        pool.dma_reset(range(s.num, s.num + 1))
                        pool.sem_clear(s)

    src_bucket = dram("src_bucket", [EP], BF16)
    dst_bucket = dram("dst_bucket", [EP], BF16)
    src_lo = dram("src_lo", [EP])
    dst_lo = dram("dst_lo", [EP])
    by_src = dram("by_src", [P, TT, SR])
    by_dst = dram("by_dst", [P, TT, DR])
    dst_meta = dram("dst_meta", [P, TILES, 2])
    hid_t = dram("hid_t", [P, TILES * P])
    edge_h1 = dram("edge_h1", [P, TILES * D])
    edge_h2 = dram("edge_h2", [P, TILES * D])
    table = dram("table", [N + 1, D])
    wide_table = dram("wide_table", [N + 1, 2 * D])

    def nodes(t):
        return t[0:N, :].rearrange("(l b) f -> l b f", b=NB)

    with top:
        def sb(name, shape, dt=F32):
            return top.enter_context(nc.sbuf_tensor(name, shape, dt))

        ident = sb("ident", [P, P])
        ones = sb("ones", [P, P])
        ones_b = sb("ones_b", [P, 1], BF16)
        iota_lo = sb("iota_lo", [P, LO])
        iota_b16 = sb("iota_b16", [P, P], BF16)
        iota_p = sb("iota_p", [P, 1])
        before = sb("before", [P, P])
        same_f = sb("same_f", [P, P])
        eps_t = sb("eps_t", [P, 1])
        X = sb("X", [LO, W])
        ACC = sb("ACC", [LO, W])
        deg = sb("deg", [LO, NB])
        start_s = sb("start_s", [P, 1])
        start_d = sb("start_d", [P, 1])
        off_s = sb("off_s", [1, TILES], I32)
        off_d = sb("off_d", [1, TILES], I32)

        with Phase('const') as ph:
            ramp = ph.sb("ramp", [P, P])
            filled, made, done = ph.sem("filled"), ph.sem("made"), ph.sem("done")
            x_in = ph.sem("x_in")
            with nc.Block() as block:
                @block.sync
                def _(sp):
                    sp.dma_start(X[:, :], nodes(a["x"]).rearrange("l b f -> l (b f)")).then_inc(x_in, 16)
                    sp.dma_start(table[:, :], a["x"][:, :]).then_inc(x_in, 16)
                    sp.dma_start(wide_table[N:N + 1, :],
                                 a["zeros"][0:1, 0:2 * D]).then_inc(x_in, 16)
                    sp.wait_ge(x_in, 48)
                    sp.wait_ge(made, 4)
                    for i in range(4):
                        for j in range(4):
                            sp.dma_start(same_f[i * D:(i + 1) * D, j * D:(j + 1) * D],
                                         ident[0:D, 0:D]).then_inc(done, 16)
                    sp.wait_ge(done, 16 * 16)

                @block.gpsimd
                def _(pool):
                    pool.memset(ident[:, :], 0.0).then_inc(filled, 1)
                    pool.memset(before[:, :], 0.0).then_inc(filled, 1)
                    pool.wait_ge(filled, 2)
                    pool.affine_select(out=ident[:, :], in_=ident[:, :], compare_op=ALU.not_equal, fill=1.0,
                                       base=0, pattern=[[-1, P]], channel_multiplier=1).then_inc(made, 1)
                    pool.affine_select(out=before[:, :], in_=before[:, :], compare_op=ALU.is_ge, fill=1.0,
                                       base=0, pattern=[[-1, P]], channel_multiplier=1).then_inc(made, 1)
                    pool.iota(ramp[:, :], [[1, P]], base=0, channel_multiplier=0,
                              allow_small_or_imprecise_dtypes=True).then_inc(made, 1)
                    pool.iota(iota_p[:, :], [[0, 1]], base=0, channel_multiplier=1,
                              allow_small_or_imprecise_dtypes=True).then_inc(made, 1)

                @block.vector
                def _(dve):
                    dve.memset(ones[:, :], 1.0)
                    dve.memset(ones_b[:, :], 1.0)
                    dve.memset(eps_t[:, :], EPS)
                    dve.memset(ACC[:, :], 0.0)
                    dve.memset(deg[:, :], 0.0)
                    dve.wait_ge(made, 4)
                    dve.tensor_copy(iota_lo[:, :], ramp[:, 0:LO])
                    dve.tensor_copy(iota_b16[:, :], ramp[:, :])
                    dve.memset(before[:, NB:P], 0.0)
            ph.end()

        with Phase('keys') as ph:
            node = [ph.sb(f"node{k}", [P, COLS], I32) for k in range(2)]
            nf = ph.sb("nf", [P, COLS])
            qi = ph.sb("qi", [P, COLS], I32)
            fix = ph.sb("fix", [P, COLS])
            lo = [ph.sb(f"lo{k}", [P, COLS]) for k in range(2)]
            bucket = [ph.sb(f"bucket{k}", [P, COLS]) for k in range(2)]
            lo16 = [ph.sb(f"lo16{k}", [P, COLS], BF16) for k in range(2)]
            bucket16 = [ph.sb(f"bucket16{k}", [P, COLS], BF16) for k in range(2)]
            loaded, keyed, kept = ph.sem("loaded"), ph.sem("keyed"), ph.sem("kept")
            with nc.Block() as block:
                @block.sync
                def _(sp):
                    for k, name in enumerate(("src", "dst")):
                        sp.dma_start(node[k][:, :], a[name].rearrange("(p c) -> p c", p=P)).then_inc(loaded, 16)
                    for k, (bd, ld) in enumerate(((src_bucket, src_lo), (dst_bucket, dst_lo))):
                        sp.wait_ge(keyed, k + 1)
                        sp.dma_start(bd.rearrange("(p c) -> p c", p=P), bucket16[k][:, :]).then_inc(kept, 16)
                        sp.dma_start(ld.rearrange("(p c) -> p c", p=P), lo[k][:, :]).then_inc(kept, 16)
                    sp.wait_ge(kept, 64)

                @block.vector
                def _(dve):
                    dve.wait_ge(loaded, 32)
                    for k in range(2):
                        dve.tensor_copy(nf[:, :], node[k][:, :])
                        dve.drain()
                        dve.tensor_scalar(qi[:, :], nf[:, :], 1.0 / NB, None, ALU.mult)
                        dve.drain()
                        dve.tensor_copy(lo[k][:, :], qi[:, :])
                        dve.drain()
                        dve.scalar_tensor_tensor(out=bucket[k][:, :], in0=lo[k][:, :], scalar=-float(NB),
                                                 in1=nf[:, :], op0=ALU.mult, op1=ALU.add)
                        dve.drain()
                        dve.tensor_scalar(fix[:, :], bucket[k][:, :], 0.0, None, ALU.is_lt)
                        dve.drain()
                        dve.tensor_tensor(lo[k][:, :], lo[k][:, :], fix[:, :], ALU.subtract)
                        dve.drain()
                        dve.scalar_tensor_tensor(out=bucket[k][:, :], in0=fix[:, :], scalar=float(NB),
                                                 in1=bucket[k][:, :], op0=ALU.mult, op1=ALU.add)
                        dve.drain()
                        dve.tensor_scalar(fix[:, :], bucket[k][:, :], float(NB), None, ALU.is_ge)
                        dve.drain()
                        dve.tensor_tensor(lo[k][:, :], lo[k][:, :], fix[:, :], ALU.add)
                        dve.drain()
                        dve.scalar_tensor_tensor(out=bucket[k][:, :], in0=fix[:, :], scalar=-float(NB),
                                                 in1=bucket[k][:, :], op0=ALU.mult, op1=ALU.add)
                        dve.drain()
                        dve.tensor_scalar(fix[:, :], nf[:, :], float(N), float(NB), ALU.is_ge, ALU.mult)
                        dve.drain()
                        dve.tensor_tensor(bucket[k][:, :], bucket[k][:, :], fix[:, :], ALU.add)
                        dve.drain()
                        dve.tensor_copy(lo16[k][:, :], lo[k][:, :])
                        dve.drain()
                        dve.tensor_copy(bucket16[k][:, :], bucket[k][:, :]).then_inc(keyed, 1)
            ph.end()

            HG = 16
            HN = COLS // HG
            hit_lo = [ph.sb(f"hit_lo{s}", [P, HG, LO], BF16) for s in range(2)]
            hit_b = [[ph.sb(f"hit_b{k}{s}", [P, HG, NB], BF16) for s in range(2)] for k in range(2)]
            total = [ph.sb(f"total{k}", [NB, 1]) for k in range(2)]
            p_deg = [ph.ps(f"p_deg{s}", [P, 512]) for s in range(2)]
            p_tot = [ph.ps(f"p_tot{s}", [P, 512]) for s in range(2)]
            hits, counted, summed = ph.sem("hits"), ph.sem("counted"), ph.sem("summed")
            with nc.Block() as block:
                @block.vector
                def _(dve):
                    for k in range(2):
                        dve.memset(total[k][:, :], 0.0)
                    dve.drain().then_inc(summed, 2)

                    def add(n, s):
                        dve.wait_ge(counted, n + 1)
                        dve.wait_ge(summed, n + 2)
                        dve.tensor_tensor(deg[:, :], deg[:, :], p_deg[s][0:LO, 0:NB], ALU.add)
                        for k in range(2):
                            ins = dve.tensor_tensor(total[k][:, :], total[k][:, :], p_tot[s][0:NB, k:k + 1], ALU.add)
                        ins.then_inc(summed, 1)

                    def find(n, s):
                        cols = bass.ds(n * HG, HG)
                        wide = [P, HG, LO]
                        dve.tensor_tensor(hit_lo[s][:, :, :], iota_b16[:, None, 0:LO].broadcast_to(wide),
                                          lo16[1][:, cols][:, :, None].broadcast_to(wide), ALU.is_equal)
                        wide = [P, HG, NB]
                        for k in range(2):
                            ins = dve.tensor_tensor(hit_b[k][s][:, :, :], iota_b16[:, None, 0:NB].broadcast_to(wide),
                                                    bucket16[k][:, cols][:, :, None].broadcast_to(wide), ALU.is_equal)
                        ins.then_inc(hits, 1)

                    find(0, 0)
                    find(1, 1)
                    with dve.Fori(0, HN // 2 - 1) as i:
                        for s in range(2):
                            add(i * 2 + s, s)
                            find(i * 2 + (s + 2), s)
                    add(HN - 2, 0)
                    add(HN - 1, 1)

                @block.tensor
                def _(pe):
                    with pe.Fori(0, HN // 2) as i:
                        for s in range(2):
                            pe.wait_ge(hits, i * 2 + (s + 1))
                            pe.wait_ge(summed, i * 2 + (s + 1))
                            for t in range(HG):
                                first, last = t == 0, t == HG - 1
                                pe.matmul(p_deg[s][0:LO, 0:NB], hit_lo[s][:, t, :], hit_b[1][s][:, t, :],
                                          start=first, stop=last)
                            for k in range(2):
                                for t in range(HG):
                                    ins = pe.matmul(p_tot[s][0:NB, k:k + 1], hit_b[k][s][:, t, :], ones_b[:, :],
                                                    start=t == 0, stop=t == HG - 1)
                            ins.then_inc(counted, 1)
            ph.end()

            tiles_i = ph.sb("tiles_i", [NB, 2], I32)
            tiles_f = ph.sb("tiles_f", [NB, 2])
            spare = ph.sb("spare", [1, P])
            tile_no = ph.sb("tile_no", [P, TILES])
            begun = ph.sb("begun", [P, TILES])
            first_t = ph.sb("first_t", [P, 2])
            p_first = p_deg[0]
            p_row = [p_deg[1], p_tot[0], p_tot[1], ph.ps("p_row3", [P, 512])]
            RW = TILES // 4
            tiled, firsts, begun_s, rows_s, ramp_s = (ph.sem(n) for n in
                                                      ("tiled", "firsts", "begun_s", "rows_s", "ramp_s"))
            with nc.Block() as block:
                @block.gpsimd
                def _(pool):
                    pool.iota(tile_no[:, :], [[1, TILES]], base=0, channel_multiplier=0,
                              allow_small_or_imprecise_dtypes=True).then_inc(ramp_s, 1)

                @block.tensor
                def _(pe):
                    pe.wait_ge(tiled, 1)
                    pe.matmul(p_first[:, 0:2], before[0:NB, :], tiles_f[:, :], start=True, stop=False)
                    pe.matmul(p_first[:, 0:2], spare[:, :], ones[0:1, 0:2], start=False, stop=True).then_inc(firsts, 1)
                    for k in range(2):
                        pe.wait_ge(begun_s, 1 + 2 * k)
                        for c in range(4):
                            ins = pe.matmul(p_row[c][0:1, 0:RW], ones[0:NB, 0:1], begun[0:NB, c * RW:(c + 1) * RW],
                                            start=True, stop=True)
                        ins.then_inc(rows_s, 1)

                @block.vector
                def _(dve):
                    dve.memset(spare[:, :], 0.0)
                    dve.drain()
                    dve.memset(spare[:, NB:P], float(TILES))
                    for k in range(2):
                        dve.tensor_scalar(tiles_i[:, k:k + 1], total[k][:, :], float(P - 1), None, ALU.add)
                    dve.drain()
                    dve.tensor_scalar(tiles_i[:, :], tiles_i[:, :], 7, None, ALU.arith_shift_right)
                    dve.drain()
                    dve.tensor_copy(tiles_f[:, :], tiles_i[:, :]).then_inc(tiled, 1)
                    dve.wait_ge(firsts, 1)
                    dve.tensor_copy(first_t[:, :], p_first[:, 0:2])
                    dve.drain()
                    dve.tensor_scalar(start_s[:, :], first_t[:, 0:1], float(P), None, ALU.mult)
                    dve.tensor_scalar(start_d[:, :], first_t[:, 1:2], float(P), None, ALU.mult)
                    dve.wait_ge(ramp_s, 1)
                    for k, off in enumerate((off_s, off_d)):
                        dve.tensor_scalar(begun[:, :], tile_no[:, :], first_t[:, k:k + 1], None,
                                          ALU.is_ge).then_inc(begun_s, 1)
                        dve.wait_ge(rows_s, k + 1)
                        for c in range(4):
                            ins = dve.tensor_scalar(off[:, c * RW:(c + 1) * RW], p_row[c][0:1, 0:RW], -1.0, float(D),
                                                    ALU.add, ALU.mult)
                        ins.then_inc(begun_s, 1)
            ph.end()

        def order(other, bucket_d, lo_d, recs, R, start):
            FILL = max(f for f in range(1, 64) if TT % f == 0)
            FILLS = TT // FILL
            K = NB + 1
            with Phase('order_' + other) as ph:
                bk = [ph.sb(f"bk{s}", [P, CHUNK], BF16) for s in range(2)]
                hit = ph.sb("hit", [P, CHUNK], BF16)
                count = ph.sb("count", [P, CHUNK])
                carry = ph.sb("carry", [P, 1])
                pos = ph.sb("pos", [P, CC], I32)
                row = ph.sb("row", [P, CC], I32)
                idx = [ph.sb(f"idx{s}", [P, CC], I32) for s in range(2)]
                rec = [ph.sb(f"rec{s}", [P, CC, R]) for s in range(2)]
                far = [ph.sb(f"far{s}", [P, CC], I32) for s in range(2)]
                lot = [ph.sb(f"lot{s}", [P, CC]) for s in range(2)]
                wgt = [ph.sb(f"wgt{s}", [P, CC]) for s in range(2)]
                empty = ph.sb("empty", [P, FILL, R])
                p_pos = ph.ps("p_pos", [P, 512])
                keys_in = [ph.sem(f"keys_in{s}") for s in range(2)]
                rec_in = [ph.sem(f"rec_in{s}") for s in range(2)]
                sent = [ph.sem(f"sent{s}") for s in range(2)]
                keys_free, placed, begun, ranked, indexed, packed, free, blank, filled = (
                    ph.sem(n) for n in ("keys_free", "placed", "begun", "ranked", "indexed", "packed", "free",
                                        "blank", "filled"))

                def chunk(ap, c):
                    return ap[bass.ds(c * CHUNK, CHUNK)]

                with nc.Block() as block:
                    @block.sync
                    def _(sp):
                        sp.wait_ge(blank, 1)
                        for f in range(FILLS):
                            sp.dma_start(recs[:, f * FILL:(f + 1) * FILL, :], empty[:, :, :]).then_inc(filled, 16)
                        with sp.Fori(0, NCH // 2) as i:
                            for s in range(2):
                                c = i * 2 + s
                                sp.wait_ge(keys_free, c + 1)
                                sp.sem_inc(begun, 1)
                                sp.dma_start(bk[s][0:K, :],
                                             chunk(bucket_d, c)[None, :].broadcast_to([K, CHUNK])).then_inc(keys_in[s], 16)
                                sp.wait_ge(free, c + 1)
                                sp.sem_inc(begun, 1)
                                for to, of in ((far[s], a[other]), (lot[s], lo_d)):
                                    sp.dma_start(to[:, :], chunk(of, c).rearrange("(p t) -> p t", t=CC)).then_inc(rec_in[s], 16)
                                if R == SR:
                                    of = chunk(a["edge_weight"], c).rearrange("(p t) -> p t", t=CC)
                                    sp.dma_start(wgt[s][:, :], of).then_inc(rec_in[s], 16)
                                else:
                                    of = a["edge_attr_32"][bass.ds(c * CHUNK, CHUNK), :].rearrange("(p t) f -> p t f", t=CC)
                                    sp.dma_start(rec[s][:, :, 2:R], of).then_inc(rec_in[s], 16)
                        sp.wait_ge(filled, 16 * FILLS)

                    @block.vector
                    def _(dve):
                        dve.memset(empty[:, :, :], 0.0)
                        dve.drain()
                        dve.memset(empty[:, :, 0:1].bitcast(I32), N)
                        dve.memset(empty[:, :, 1:2], -1.0).then_inc(blank, 1)
                        for s in range(2):
                            dve.memset(rec[s][:, :, :], 0.0)
                        dve.tensor_copy(carry[:, :], start[:, :]).then_inc(keys_free, 2)
                        with dve.Fori(0, NCH // 2) as i:
                            for s in range(2):
                                c = i * 2 + s
                                dve.wait_ge(keys_in[s], i * 16 + 16)
                                dve.tensor_scalar(hit[0:K, :], bk[s][0:K, :], iota_p[0:K, :], None,
                                                  ALU.is_equal).then_inc(keys_free, 1)
                                dve.drain()
                                dve.tensor_tensor_scan(count[0:K, :], hit[0:K, :], hit[0:K, :], carry[0:K, :],
                                                       ALU.add, ALU.max)
                                dve.drain()
                                dve.tensor_copy(carry[0:K, :], count[0:K, CHUNK - 1:CHUNK])
                                dve.drain()
                                dve.tensor_tensor(count[0:K, :], count[0:K, :], hit[0:K, :],
                                                  ALU.mult).then_inc(placed, 1)
                                dve.drain()
                                dve.wait_ge(ranked, c + 1)
                                dve.tensor_scalar(pos[:, :], p_pos[:, 0:CC], -1.0, None, ALU.add)
                                dve.drain()
                                dve.tensor_scalar(row[:, :], pos[:, :], P - 1, None, ALU.bitwise_and)
                                dve.tensor_scalar(pos[:, :], pos[:, :], 7, None, ALU.arith_shift_right)
                                dve.drain()
                                dve.wait_ge(free, c + 1)
                                dve.scalar_tensor_tensor(out=idx[s][:, :], in0=row[:, :], scalar=float(TT),
                                                         in1=pos[:, :], op0=ALU.mult, op1=ALU.add).then_inc(indexed, 1)

                    @block.tensor
                    def _(pe):
                        by_col = count[0:K, :].rearrange("k (p t) -> k t p", t=CC)
                        with pe.Fori(0, NCH) as c:
                            pe.wait_ge(placed, c + 1)
                            for t in range(CC):
                                ins = pe.matmul(p_pos[:, t:t + 1], by_col[:, t, :], ones[0:K, 0:1],
                                                start=True, stop=True)
                            ins.then_inc(ranked, 1)

                    @block.scalar
                    def _(act):
                        with act.Fori(0, NCH // 2) as i:
                            for s in range(2):
                                act.wait_ge(rec_in[s], i * 48 + 48)
                                ins = act.copy(rec[s][:, :, 0].bitcast(I32), far[s][:, :])
                                if R == SR:
                                    act.copy(rec[s][:, :, 2], wgt[s][:, :])
                                act.copy(rec[s][:, :, 1], lot[s][:, :]).then_inc(packed, 1)

                    @block.gpsimd
                    def _(pool):
                        rows = recs.rearrange("p t r -> (p t) r")

                        def send(i, s, first=False):
                            pool.wait_ge(indexed, i * 2 + (s + 1))
                            pool.wait_ge(packed, i * 2 + (s + 1))
                            pool.wait_ge(filled, 16 * FILLS)
                            pool.sem_inc(begun, 1)
                            for t in range(CC):
                                pool.indirect_dma_start(rows, bass.IndirectOffsetOnAxis(ap=idx[s][:, t:t + 1], axis=0),
                                                        rec[s][:, t, :], None).then_inc(sent[s], 16)
                            if not first:
                                pool.wait_ge(sent[1 - s], (i + s) * (16 * CC))
                                pool.sem_inc(free, 1)

                        pool.sem_inc(free, 2)
                        send(0, 0, first=True)
                        send(0, 1)
                        with pool.Fori(1, NCH // 2) as i:
                            send(i, 0)
                            send(i, 1)
                        pool.wait_ge(sent[1], NCH // 2 * 16 * CC)
                ph.end()

        order("src", dst_bucket, dst_lo, by_dst, DR, start_d)
        order("dst", src_bucket, src_lo, by_src, SR, start_s)
        TMP = sb("TMP", [LO, W])
        add_regs = [nc.vector.alloc_register(f"add_at{j}") for j in range(G)]
        row_regs = [nc.tensor.alloc_register(f"row_at{j}") for j in range(G)]

        def blocks(name, rows, cols, parts, of):
            t = sb(name, [rows * parts, cols * parts])
            weights.append((t, [(t[n * rows:(n + 1) * rows, n * cols:(n + 1) * cols], of) for n in range(parts)]))
            return t

        def column(name, parts, of):
            size = of.shape[0]
            t = sb(name, [size * parts, 1])
            weights.append((t, [(t[n * size:(n + 1) * size, :], of[:, None]) for n in range(parts)]))
            return t

        def across(name, of, rows=P):
            size = of.shape[0]
            t = sb(name, [rows, size])
            weights.append((t, [(t[:, :], of[None, :].broadcast_to([rows, size]))]))
            return t

        weights = []
        w0 = blocks("w0", D, D, 4, a["L0_gnn_weight"])
        w1a = blocks("w1a", D, D, 4, a["L1_gnn_W1"][0:D, :])
        w1b = blocks("w1b", D, D, 4, a["L1_gnn_W1"][D:2 * D, :])
        w12 = blocks("w12", D, D, 4, a["L1_gnn_W2"])
        b1c, g1c, be1c = (column(n, 4, a[f"L1_gnn_{n}"]) for n in ("b1", "gamma1", "beta1"))
        b2r, g2r, be2r = (across(n, a[f"L1_gnn_{n}"]) for n in ("b2", "gamma2", "beta2"))
        w21 = [sb(f"w21{h}", [P, P]) for h in range(2)]
        for h in range(2):
            weights.append((w21[h], [(w21[h][(2 * h + n) * D:(2 * h + n + 1) * D, n * HID:(n + 1) * HID], a["L2_gnn_W1"])
                                     for n in range(2)]))
        w22 = blocks("w22", HID, D, 2, a["L2_gnn_W2"])
        b21c = column("b21", 2, a["L2_gnn_b1"])
        b22r = across("b22", a["L2_gnn_b2"])
        lin0 = blocks("lin0", D, D, 4, a["lin0_t"])
        lin0b = across("lin0b", a["L3_gnn_lin0_b"])
        en1 = [sb(f"en1{n}", [P, EH]) for n in range(4)]
        for n in range(4):
            weights.append((en1[n], [(en1[n][n * D:(n + 1) * D, :], a["en1_t"])]))
        en1b = column("en1b", 1, a["L3_gnn_en1_b"])
        en2 = sb("en2", [EH, D * D])
        weights.append((en2, [(en2[:, :], a["en2_t"])]))
        en2b = blocks("en2b", D, D, 4, a["en2_b"])
        convb = column("convb", 4, a["L3_gnn_conv_bias"])
        wih = sb("wih", [P, 4 * P])
        whh = sb("whh", [P, 3 * P])
        gbias = sb("gbias", [2, 4 * P])
        for t, of in ((wih, a["wih_t"]), (whh, a["whh_t"])):
            weights.append((t, [(t[n * D:(n + 1) * D, k * P + n * D:k * P + (n + 1) * D], of[:, k * D:(k + 1) * D])
                                for n in range(4) for k in range(3)]))
        weights.append((gbias, [(gbias[r:r + 1, at * P + n * D:at * P + (n + 1) * D], of[None, k * D:(k + 1) * D])
                                for n in range(4) for r, of, at_n in ((0, a["L3_gnn_gru_bih"], 2),
                                                                      (1, a["L3_gnn_gru_bhh"], 3))
                                for k, at in ((0, 0), (1, 1), (2, at_n))]))

        with Phase("weights") as ph:
            zeroed, w_in = ph.sem("zeroed"), ph.sem("w_in")
            with nc.Block() as block:
                @block.vector
                def _(dve):
                    for t, _ in weights:
                        dve.memset(t[:, :], 0.0).then_inc(zeroed, 1)

                @block.sync
                def _(sp):
                    n = 0
                    for k, (_, parts) in enumerate(weights):
                        sp.wait_ge(zeroed, k + 1)
                        for to, of in parts:
                            with nc.allow_non_contiguous_dma(reason="bias columns"):
                                sp.dma_start(to, of).then_inc(w_in, 16)
                            n += 1
                    sp.wait_ge(w_in, 16 * n)
            ph.end()

        def zero_row(width):
            return a["zeros"][0:1, 0:width]

        def f3(t):
            return t[:, :].rearrange("l (b f) -> l b f", f=D)

        def per_bucket(t):
            return t[:, :, None].broadcast_to([LO, NB, D])

        def layer_norm(tag, y, to):
            with Phase(tag) as ph:
                sq = ph.sb("sq", [LO, W])
                m, v = ph.sb("m", [LO, NB]), ph.sb("v", [LO, NB])
                centred, squared, varied, rooted = (ph.sem(n) for n in ("centred", "squared", "varied", "rooted"))
                with nc.Block() as block:
                    @block.vector
                    def _(dve):
                        dve.tensor_reduce(m[:, :], f3(y), AX, ALU.add)
                        dve.drain()
                        dve.tensor_scalar(m[:, :], m[:, :], 1.0 / D, None, ALU.mult)
                        dve.drain()
                        dve.tensor_tensor(f3(y), f3(y), per_bucket(m), ALU.subtract).then_inc(centred, 1)
                        dve.wait_ge(squared, 1)
                        dve.tensor_reduce(v[:, :], f3(sq), AX, ALU.add).then_inc(varied, 1)
                        dve.wait_ge(rooted, 1)
                        dve.reciprocal(v[:, :], v[:, :])
                        dve.drain()
                        dve.tensor_tensor(f3(to), f3(y), per_bucket(v), ALU.mult)

                    @block.scalar
                    def _(act):
                        act.wait_ge(centred, 1)
                        act.activation(sq[:, :], y[:, :], ACT.Square).then_inc(squared, 1)
                        act.wait_ge(varied, 1)
                        act.activation(v[:, :], v[:, :], ACT.Sqrt, bias=eps_t[0:LO, :],
                                       scale=1.0 / D).then_inc(rooted, 1)
                ph.end()

        def node_products(tag, source, rhs, take):
            with Phase(tag) as ph:
                turned = [ph.sb(f"turned{s}", [P, LO]) for s in range(2)]
                p_t = [ph.ps(f"p_t{s}", [P, 512]) for s in range(2)]
                p_o = [[ph.ps(f"p_o{s}{k}", [P, 512]) for k in range(len(rhs))] for s in range(2)]
                t_ok, c_ok, o_ok, taken = (ph.sem(n) for n in ("t_ok", "c_ok", "o_ok", "taken"))
                with nc.Block() as block:
                    @block.tensor
                    def _(pe):
                        def turn(q):
                            if q >= 2:
                                pe.wait_ge(c_ok, q - 1)
                            pe.transpose(p_t[q % 2][:, 0:LO], source[:, q * P:(q + 1) * P],
                                         ident[0:LO, 0:LO]).then_inc(t_ok, 1)

                        turn(0)
                        for q in range(Q):
                            if q + 1 < Q:
                                turn(q + 1)
                            pe.wait_ge(c_ok, q + 1)
                            if q >= 2:
                                pe.wait_ge(taken, q - 1)
                            for k, w in enumerate(rhs):
                                ins = pe.matmul(p_o[q % 2][k][0:LO, 0:P], turned[q % 2][:, :], w[:, :],
                                                start=True, stop=True)
                            ins.then_inc(o_ok, 1)

                    @block.scalar
                    def _(act):
                        for q in range(Q):
                            act.wait_ge(t_ok, q + 1)
                            if q >= 2:
                                act.wait_ge(o_ok, q - 1)
                            act.copy(turned[q % 2][:, :], p_t[q % 2][:, 0:LO]).then_inc(c_ok, 1)

                    @block.vector
                    def _(dve):
                        for q in range(Q):
                            dve.wait_ge(o_ok, q + 1)
                            take(dve, q, [p[0:LO, 0:P] for p in p_o[q % 2]]).then_inc(taken, 1)
                ph.end()

        def store_table(tag, parts):
            with Phase(tag) as ph:
                stored = ph.sem("stored")
                with nc.Block() as block:
                    @block.sync
                    def _(sp):
                        for to, of in parts:
                            sp.dma_start(to, of).then_inc(stored, 16)
                        sp.wait_ge(stored, 16 * len(parts))
                ph.end()

        def clear(t):
            with nc.Block() as block:
                @block.vector
                def _(dve):
                    dve.memset(t[:, :], 0.0)

        AHEAD = 2 * G

        def add_sums(dve, ph_added, summed, p_sum, off, acc, g, s):
            dve.load(add_regs, off[0:1, bass.ds(g * G, G)])
            dve.wait_ge(summed, g + 3)
            for j in range(G):
                at = dve.snap(add_regs[j], min_val=0, max_val=W - D)
                to = acc[0:LO, bass.ds(at, D)]
                dve.wait_ge(ph_added, g * G + (j + AHEAD))
                dve.tensor_tensor(to, to, p_sum[s][0:LO, j * D:(j + 1) * D], ALU.add).then_inc(ph_added, 1)

        class EdgeNetwork:

            def __init__(self, ph):
                self.rec = [ph.sb(f"rec{s}", [P, G, DR]) for s in range(2)]
                self.head = [ph.sb(f"head{s}", [P, G, 2]) for s in range(2)]
                self.attr = [ph.sb(f"attr{s}", [P, GD]) for s in range(2)]
                self.attr_t = [ph.sb(f"attr_t{s}", [P, 4 * P]) for s in range(2)]
                self.hid = [ph.sb(f"hid{s}", [P, G * P]) for s in range(2)]
                self.p_t = [ph.ps(f"p_t{s}", [P, 512]) for s in range(2)]
                self.p_e = [ph.ps(f"p_e{n}", [P, 512]) for n in range(4)]
                self.rec_in = [ph.sem(f"rec_in{s}") for s in range(2)]
                self.kept = [ph.sem(f"kept{s}") for s in range(2)]
                self.parted, self.turned, self.copied, self.mapped, self.relued, self.fetched, self.storing = (
                    ph.sem(n) for n in ("parted", "turned", "copied", "mapped", "relued", "fetched", "storing"))

            def start_sp(self, sp):
                for s in range(2):
                    sp.sem_inc(self.kept[s], 32)

            def start_dve(self, dve):
                dve.sem_inc(self.parted, 2)

            def start_act(self, act):
                act.sem_inc(self.copied, 2)
                act.sem_inc(self.relued, 4)
                act.sem_inc(self.mapped, 8)

            def fetch(self, sp, i, s):
                g = i * 2 + s
                sp.wait_ge(self.parted, g + 1)
                sp.sem_inc(self.fetched, 1)
                sp.dma_start(self.rec[s][:, :, :], by_dst[:, bass.ds(g * G, G), :]).then_inc(self.rec_in[s], 16)

            def store(self, sp, i, s):
                g = i * 2 + s
                sp.wait_ge(self.relued, g * 4 + 8)
                sp.sem_inc(self.storing, 1)
                sp.dma_start(dst_meta[:, bass.ds(g * G, G), :], self.head[s][:, :, :]).then_inc(self.kept[s], 16)
                sp.dma_start(hid_t[:, bass.ds(g * (G * P), G * P)], self.hid[s][:, :]).then_inc(self.kept[s], 16)

            def end(self, sp):
                for s in range(2):
                    sp.wait_ge(self.kept[s], NG // 2 * 32 + 32)

            def part(self, dve, i, s):
                dve.wait_ge(self.rec_in[s], i * 16 + 16)
                dve.wait_ge(self.copied, i * 2 + (s + 1))
                dve.wait_ge(self.kept[s], i * 32 + 32)
                dve.tensor_copy(self.attr[s][:, :].rearrange("p (t f) -> p t f", f=D), self.rec[s][:, :, 2:DR])
                dve.tensor_copy(self.head[s][:, :, :], self.rec[s][:, :, 0:2]).then_inc(self.parted, 1)

            def turn(self, pe, i, s):
                g = i * 2 + s
                pe.wait_ge(self.parted, g + 3)
                pe.wait_ge(self.copied, g + 1)
                for k in range(4):
                    ins = pe.transpose(self.p_t[s][:, k * P:(k + 1) * P], self.attr[s][:, k * P:(k + 1) * P], ident[:, :])
                ins.then_inc(self.turned, 1)

            def times(self, pe, i, s):
                g = i * 2 + s
                pe.wait_ge(self.copied, g + 3)
                for n in range(4):
                    pe.wait_ge(self.relued, g * 4 + (n + 1))
                    pe.matmul(self.p_e[n][:, :], en1[n][:, :], self.attr_t[s][:, :],
                              start=True, stop=True).then_inc(self.mapped, 1)

            def copy(self, act, i, s):
                g = i * 2 + s
                act.wait_ge(self.turned, g + 1)
                act.wait_ge(self.mapped, g * 4 + 4)
                act.copy(self.attr_t[s][:, :], self.p_t[s][:, :]).then_inc(self.copied, 1)

            def relu(self, act, i, s):
                g = i * 2 + s
                to = self.hid[s][:, :].rearrange("p (k n e) -> p n k e", k=4, n=4)
                act.wait_ge(self.kept[s], i * 32 + 32)
                for n in range(4):
                    act.wait_ge(self.mapped, g * 4 + (n + 9))
                    act.activation(to[:, n, :, :], self.p_e[n][:, :].rearrange("p (k e) -> p k e", k=4), ACT.Relu,
                                   bias=en1b[:, :]).then_inc(self.relued, 1)

        def gather_sum(tag, meta, mr, tab, weighted, off, acc, edges=False):
            with Phase(tag) as ph:
                net = EdgeNetwork(ph) if edges else None
                mt = [ph.sb(f"mt{s}", [P, G, mr]) for s in range(2)]
                xg = [ph.sb(f"xg{s}", [P, G, D]) for s in range(2)]
                hit = [ph.sb(f"hit{s}", [P, G, LO]) for s in range(2)]
                p_sum = [ph.ps(f"p_sum{s}", [P, 512]) for s in range(2)]
                meta_in = [ph.sem(f"meta_in{s}") for s in range(2)]
                rows_in = [ph.sem(f"rows_in{s}") for s in range(2)]
                hits, summed, added, begun = (ph.sem(n) for n in ("hits", "summed", "added", "begun"))
                with nc.Block() as block:
                    @block.sync
                    def _(sp):
                        def fetch(i, s):
                            sp.wait_ge(summed, i * 2 + (s + 1))
                            sp.sem_inc(begun, 1)
                            sp.dma_start(mt[s][:, :, :], meta[:, bass.ds((i * 2 + s) * G, G), :]).then_inc(meta_in[s], 16)
                            if net:
                                net.fetch(sp, i, s)

                        def store(i, s):
                            if net:
                                net.store(sp, i, s)

                        if net:
                            net.start_sp(sp)
                        fetch(0, 0)
                        with sp.Fori(0, NG // 2 - 1) as i:
                            fetch(i, 1)
                            store(i, 0)
                            fetch(i + 1, 0)
                            store(i, 1)
                        fetch(NG // 2 - 1, 1)
                        store(NG // 2 - 1, 0)
                        store(NG // 2 - 1, 1)
                        if net:
                            net.end(sp)

                    if net:
                        @block.scalar
                        def _(act):
                            net.start_act(act)
                            with act.Fori(0, NG // 2) as i:
                                for s in range(2):
                                    net.copy(act, i, s)
                                    net.relu(act, i, s)

                    @block.gpsimd
                    def _(pool):
                        with pool.Fori(0, NG // 2) as i:
                            for s in range(2):
                                pool.wait_ge(meta_in[s], i * 16 + 16)
                                pool.wait_ge(summed, i * 2 + (s + 1))
                                pool.sem_inc(begun, 1)
                                for j in range(G):
                                    pool.indirect_dma_start(
                                        xg[s][:, j, :], None, tab[:, :],
                                        bass.IndirectOffsetOnAxis(ap=mt[s][:, j, 0:1].bitcast(I32), axis=0)).then_inc(rows_in[s], 16)

                    @block.vector
                    def _(dve):
                        def find(i, s):
                            dve.wait_ge(meta_in[s], i * 16 + 16)
                            dve.wait_ge(summed, i * 2 + (s + 1))
                            for j in range(G):
                                if weighted:
                                    ins = dve.tensor_scalar(hit[s][:, j, :], iota_lo[:, :], mt[s][:, j, 1:2],
                                                            mt[s][:, j, 2:3], ALU.is_equal, ALU.mult)
                                else:
                                    ins = dve.tensor_scalar(hit[s][:, j, :], iota_lo[:, :], mt[s][:, j, 1:2],
                                                            None, ALU.is_equal)
                            ins.then_inc(hits, 1)
                            if net:
                                net.part(dve, i, s)

                        if net:
                            net.start_dve(dve)
                        dve.sem_inc(added, AHEAD)
                        find(0, 0)
                        with dve.Fori(0, NG // 2 - 1) as i:
                            find(i, 1)
                            add_sums(dve, added, summed, p_sum, off, acc, i * 2, 0)
                            find(i + 1, 0)
                            add_sums(dve, added, summed, p_sum, off, acc, i * 2 + 1, 1)
                        find(NG // 2 - 1, 1)
                        add_sums(dve, added, summed, p_sum, off, acc, NG - 2, 0)
                        add_sums(dve, added, summed, p_sum, off, acc, NG - 1, 1)

                    @block.tensor
                    def _(pe):
                        pe.sem_inc(summed, 2)
                        with pe.Fori(0, NG // 2) as i:
                            for s in range(2):
                                if net:
                                    net.turn(pe, i, s)
                                pe.wait_ge(hits, i * 2 + (s + 1))
                                pe.wait_ge(rows_in[s], i * (16 * G) + 16 * G)
                                pe.wait_ge(added, (i * 2 + s) * G + G)
                                for j in range(G):
                                    ins = pe.matmul(p_sum[s][0:LO, j * D:(j + 1) * D], hit[s][:, j, :], xg[s][:, j, :],
                                                    start=True, stop=True)
                                ins.then_inc(summed, 1)
                                if net:
                                    net.times(pe, i, s)
                ph.end()

        gather_sum("l0", by_src, SR, table, True, off_s, ACC, edges=True)

        def plus_x(dve, q, p):
            cols = slice(q * P, (q + 1) * P)
            return dve.tensor_tensor(TMP[:, cols], X[:, cols], p[0], ALU.add)

        node_products("l0w", ACC, [w0], plus_x)
        layer_norm("l0n", TMP, X)
        def halves(dve, q, p):
            cols = slice(q * P, (q + 1) * P)
            dve.tensor_copy(TMP[:, cols], p[0])
            return dve.tensor_copy(ACC[:, cols], p[1])

        node_products("l1h", X, [w1a, w1b], halves)
        store_table("l1t", [(nodes(table), f3(ACC)), (table[N:N + 1, :], zero_row(D))])

        sums = sb("sums", [P, GD])
        squares = sb("squares", [P, GD])
        scale1, shift1 = sb("scale1", [P, 1]), sb("shift1", [P, 1])
        scale2, shift2 = sb("scale2", [P, D]), sb("shift2", [P, D])

        def tally(dve, v, sq, squared, n):
            dve.tensor_tensor(sums[:, :], sums[:, :], v, ALU.add)
            dve.wait_ge(squared, n)
            return dve.tensor_tensor(squares[:, :], squares[:, :], sq, ALU.add)

        with Phase("l1a") as ph:
            mt = [ph.sb(f"mt{s}", [P, G, SR]) for s in range(2)]
            xg = [ph.sb(f"xg{s}", [P, GD]) for s in range(2)]
            hit = [ph.sb(f"hit{s}", [P, G, LO]) for s in range(2)]
            hit_t = [ph.sb(f"hit_t{s}", [LO, 4 * P]) for s in range(2)]
            h = [ph.sb(f"h{s}", [P, GD]) for s in range(2)]
            sq = [ph.sb(f"sq{s}", [P, GD]) for s in range(2)]
            p_t = [ph.ps(f"p_t{s}", [P, 512]) for s in range(2)]
            p_h = [ph.ps(f"p_h{s}", [P, 512]) for s in range(2)]
            meta_in = [ph.sem(f"meta_in{s}") for s in range(2)]
            rows_in = [ph.sem(f"rows_in{s}") for s in range(2)]
            stored = [ph.sem(f"stored{s}") for s in range(2)]
            hits, turned, copied, near, ready, squared, tallied, begun, kept = (ph.sem(n) for n in (
                "hits", "turned", "copied", "near", "ready", "squared", "tallied", "begun", "kept"))
            with nc.Block() as block:
                @block.sync
                def _(sp):
                    def fetch(g, s):
                        sp.dma_start(mt[s][:, :, :], by_src[:, bass.ds(g * G, G), :]).then_inc(meta_in[s], 16)

                    sp.sem_inc(kept, 2)
                    with sp.Fori(0, NG // 2) as i:
                        for s in range(2):
                            sp.wait_ge(tallied, i * 2 + (s + 1))
                            sp.sem_inc(begun, 1)
                            fetch(i * 2 + s, s)

                @block.gpsimd
                def _(pool):
                    with pool.Fori(0, NG // 2) as i:
                        for s in range(2):
                            pool.wait_ge(meta_in[s], i * 16 + 16)
                            pool.wait_ge(tallied, i * 2 + (s + 1))
                            pool.sem_inc(begun, 1)
                            for j in range(G):
                                pool.indirect_dma_start(
                                    xg[s][:, j * D:(j + 1) * D], None, table[:, :],
                                    bass.IndirectOffsetOnAxis(ap=mt[s][:, j, 0:1].bitcast(I32), axis=0)).then_inc(rows_in[s], 16)

                @block.scalar
                def _(act):
                    def store(i, s):
                        act.dma_start(edge_h1[:, bass.ds((i * 2 + s) * GD, GD)], h[s][:, :]).then_inc(stored[s], 16)

                    act.sem_inc(copied, 2)
                    with act.Fori(0, NG // 2) as i:
                        for s in range(2):
                            for k in range(G // 4):
                                n = (i * 2 + s) * (G // 4) + k
                                act.wait_ge(turned, n + 1)
                                act.wait_ge(near, n + 1)
                                act.copy(hit_t[k % 2][:, :], p_t[k % 2][0:LO, :]).then_inc(copied, 1)
                            act.wait_ge(ready, i * 2 + (s + 1))
                            act.wait_ge(tallied, i * 2 + (s + 1))
                            act.activation(sq[s][:, :], h[s][:, :], ACT.Square).then_inc(squared, 1)
                            store(i, s)

                @block.tensor
                def _(pe):
                    pe.sem_inc(near, 2)
                    with pe.Fori(0, NG // 2) as i:
                        for s in range(2):
                            g = i * 2 + s
                            pe.load(row_regs, off_s[0:1, bass.ds(g * G, G)])
                            pe.wait_ge(hits, g + 1)
                            pe.wait_ge(tallied, g + 1)

                            def turn(k):
                                pe.wait_ge(copied, g * (G // 4) + (k + 1))
                                for t in range(4):
                                    ins = pe.transpose(p_t[k % 2][0:LO, t * P:(t + 1) * P], hit[s][:, 4 * k + t, :],
                                                       ident[:, :])
                                ins.then_inc(turned, 1)

                            turn(0)
                            for k in range(G // 4):
                                if k + 1 < G // 4:
                                    turn(k + 1)
                                pe.wait_ge(copied, g * (G // 4) + (k + 3))
                                for t in range(4):
                                    j = 4 * k + t
                                    at = pe.snap(row_regs[j], min_val=0, max_val=W - D)
                                    ins = pe.matmul(p_h[s][:, j * D:(j + 1) * D], hit_t[k % 2][:, t * P:(t + 1) * P],
                                                    TMP[0:LO, bass.ds(at, D)], start=True, stop=True)
                                ins.then_inc(near, 1)

                @block.vector
                def _(dve):
                    def find(i, s):
                        dve.wait_ge(meta_in[s], i * 16 + 16)
                        dve.wait_ge(tallied, i * 2 + (s + 1))
                        for j in range(G):
                            ins = dve.tensor_scalar(hit[s][:, j, :], iota_lo[:, :], mt[s][:, j, 1:2], None, ALU.is_equal)
                        ins.then_inc(hits, 1)

                    def join(i, s, again=True):
                        g = i * 2 + s
                        dve.wait_ge(near, g * (G // 4) + (G // 4 + 2))
                        dve.wait_ge(rows_in[s], i * (16 * G) + 16 * G)
                        if again:
                            dve.wait_ge(stored[s], i * 16)
                        dve.tensor_tensor(h[s][:, :], p_h[s][:, :], xg[s][:, :], ALU.add).then_inc(ready, 1)
                        dve.wait_ge(ready, g + 1)
                        dve.wait_ge(tallied, g + 2)
                        tally(dve, h[s][:, :], sq[s][:, :], squared, g + 1).then_inc(tallied, 1)

                    dve.memset(sums[:, :], 0.0)
                    dve.memset(squares[:, :], 0.0)
                    dve.drain().then_inc(tallied, 2)
                    find(0, 0)
                    find(0, 1)
                    join(0, 0, again=False)
                    find(1, 0)
                    join(0, 1, again=False)
                    with dve.Fori(1, NG // 2 - 1) as i:
                        find(i, 1)
                        join(i, 0)
                        find(i + 1, 0)
                        join(i, 1)
                    find(NG // 2 - 1, 1)
                    join(NG // 2 - 1, 0)
                    join(NG // 2 - 1, 1)
                    for s in range(2):
                        dve.wait_ge(stored[s], NG // 2 * 16)
            ph.end()

        def norm_terms(dve, s, q, g, be, b, mean, var, root, rooted, scale, shift, varied):
            dve.tensor_scalar(mean, s, 1.0 / E, None, ALU.mult)
            dve.tensor_scalar(var, q, 1.0 / E, None, ALU.mult)
            dve.drain()
            dve.tensor_tensor(shift, mean, mean, ALU.mult)
            dve.drain()
            dve.tensor_tensor(var, var, shift, ALU.subtract)
            dve.drain()
            dve.tensor_scalar(var, var, 0.0, None, ALU.max).then_inc(varied, 1)
            dve.wait_ge(rooted, 1)
            dve.reciprocal(var, root)
            dve.tensor_tensor(mean, mean, b, ALU.add)
            dve.drain()
            dve.tensor_tensor(scale, g, var, ALU.mult)
            dve.tensor_tensor(mean, b, mean, ALU.subtract)
            dve.drain()
            dve.tensor_tensor(shift, scale, mean, ALU.mult)
            dve.drain()
            dve.tensor_tensor(shift, shift, be, ALU.add)

        with Phase("l1s") as ph:
            cols = ph.sb("cols", [P, 2])
            mean, var, root, both = (ph.sb(n, [P, w]) for n, w in (("mean", 1), ("var", 1), ("root", 1), ("both", 2)))
            p_c = ph.ps("p_c", [P, 512])
            p_f = ph.ps("p_f", [P, 512])
            summed, cols_ok, folded, varied, rooted = (ph.sem(n) for n in ("summed", "cols_ok", "folded", "varied", "rooted"))
            with nc.Block() as block:
                @block.tensor
                def _(pe):
                    for k, t in enumerate((sums, squares)):
                        for c in range(4):
                            ins = pe.matmul(p_c[:, k:k + 1], t[:, c * P:(c + 1) * P], ones[:, 0:1],
                                            start=c == 0, stop=c == 3)
                    ins.then_inc(summed, 1)
                    pe.wait_ge(cols_ok, 1)
                    pe.matmul(p_f[:, 0:2], same_f[:, :], cols[:, :], start=True, stop=True).then_inc(folded, 1)

                @block.scalar
                def _(act):
                    act.wait_ge(varied, 1)
                    act.activation(root[:, :], var[:, :], ACT.Sqrt, bias=eps_t[:, :]).then_inc(rooted, 1)

                @block.vector
                def _(dve):
                    dve.wait_ge(summed, 1)
                    dve.tensor_copy(cols[:, :], p_c[:, 0:2]).then_inc(cols_ok, 1)
                    dve.wait_ge(folded, 1)
                    dve.tensor_copy(both[:, :], p_f[:, 0:2])
                    dve.drain()
                    norm_terms(dve, both[:, 0:1], both[:, 1:2], g1c[:, :], be1c[:, :], b1c[:, :], mean[:, :], var[:, :],
                               root[:, :], rooted, scale1[:, :], shift1[:, :], varied)
            ph.end()

        with Phase("l1b") as ph:
            mt = [ph.sb(f"mt{s}", [P, G, SR]) for s in range(2)]
            h = [ph.sb(f"h{s}", [P, GD]) for s in range(2)]
            act_t = [ph.sb(f"act_t{s}", [P, 4 * P]) for s in range(2)]
            real = [ph.sb(f"real{s}", [P, G]) for s in range(2)]
            h2 = [ph.sb(f"h2{s}", [P, GD]) for s in range(2)]
            sq = [ph.sb(f"sq{s}", [P, GD]) for s in range(2)]
            p_t = [ph.ps(f"p_t{s}", [P, 512]) for s in range(2)]
            p_h = [ph.ps(f"p_h{s}", [P, 512]) for s in range(2)]
            in_ = [ph.sem(f"in_{s}") for s in range(2)]
            stored = [ph.sem(f"stored{s}") for s in range(2)]
            turned, masked, relued, mapped, ready, squared, tallied, begun = (ph.sem(n) for n in (
                "turned", "masked", "relued", "mapped", "ready", "squared", "tallied", "begun"))
            with nc.Block() as block:
                @block.sync
                def _(sp):
                    with sp.Fori(0, NG // 2) as i:
                        for s in range(2):
                            g = i * 2 + s
                            sp.wait_ge(turned, g + 1)
                            sp.wait_ge(masked, g + 1)
                            sp.sem_inc(begun, 1)
                            sp.dma_start(h[s][:, :], edge_h1[:, bass.ds(g * GD, GD)]).then_inc(in_[s], 16)
                            sp.dma_start(mt[s][:, :, :], by_src[:, bass.ds(g * G, G), :]).then_inc(in_[s], 16)

                @block.tensor
                def _(pe):
                    def turn(i, s):
                        pe.wait_ge(in_[s], i * 32 + 32)
                        pe.wait_ge(relued, i * 2 + (s + 1))
                        for k in range(4):
                            ins = pe.transpose(p_t[s][:, k * P:(k + 1) * P], h[s][:, k * P:(k + 1) * P], ident[:, :])
                        ins.then_inc(turned, 1)

                    def times(i, s):
                        g = i * 2 + s
                        pe.wait_ge(relued, g + 3)
                        pe.wait_ge(tallied, g + 1)
                        for k in range(4):
                            ins = pe.matmul(p_h[s][:, k * P:(k + 1) * P], act_t[s][:, k * P:(k + 1) * P], w12[:, :],
                                            start=True, stop=True)
                        ins.then_inc(mapped, 1)

                    pe.sem_inc(turned, 2)
                    turn(0, 0)
                    with pe.Fori(0, NG // 2 - 1) as i:
                        turn(i, 1)
                        times(i, 0)
                        turn(i + 1, 0)
                        times(i, 1)
                    turn(NG // 2 - 1, 1)
                    times(NG // 2 - 1, 0)
                    times(NG // 2 - 1, 1)

                @block.scalar
                def _(act):
                    def relu(i, s):
                        act.wait_ge(turned, i * 2 + (s + 3))
                        act.wait_ge(tallied, i * 2 + (s + 1))
                        act.activation(act_t[s][:, :], p_t[s][:, :], ACT.Relu, bias=shift1[:, :],
                                       scale=scale1[:, :]).then_inc(relued, 1)

                    def square(i, s):
                        g = i * 2 + s
                        act.wait_ge(ready, g + 1)
                        act.wait_ge(tallied, g + 1)
                        act.activation(sq[s][:, :], h2[s][:, :], ACT.Square).then_inc(squared, 1)
                        act.dma_start(edge_h2[:, bass.ds(g * GD, GD)], h2[s][:, :]).then_inc(stored[s], 16)

                    act.sem_inc(relued, 2)
                    relu(0, 0)
                    with act.Fori(0, NG // 2 - 1) as i:
                        relu(i, 1)
                        square(i, 0)
                        relu(i + 1, 0)
                        square(i, 1)
                    relu(NG // 2 - 1, 1)
                    square(NG // 2 - 1, 0)
                    square(NG // 2 - 1, 1)

                @block.vector
                def _(dve):
                    def join(i, s, again=True):
                        g = i * 2 + s
                        dve.wait_ge(in_[s], i * 32 + 32)
                        dve.tensor_scalar(real[s][:, :], mt[s][:, :, 1], 0.0, None, ALU.is_ge).then_inc(masked, 1)
                        dve.drain()
                        if again:
                            dve.wait_ge(stored[s], i * 16)
                        dve.wait_ge(mapped, g + 1)
                        dve.tensor_tensor(h2[s][:, :].rearrange("p (t f) -> p t f", f=D),
                                          p_h[s][:, :].rearrange("p (t f) -> p t f", f=D),
                                          real[s][:, :, None].broadcast_to([P, G, D]), ALU.mult).then_inc(ready, 1)
                        dve.wait_ge(ready, g + 1)
                        dve.wait_ge(tallied, g + 2)
                        tally(dve, h2[s][:, :], sq[s][:, :], squared, g + 1).then_inc(tallied, 1)

                    dve.memset(sums[:, :], 0.0)
                    dve.memset(squares[:, :], 0.0)
                    dve.memset(ACC[:, :], 0.0)
                    dve.drain().then_inc(tallied, 2)
                    dve.sem_inc(masked, 2)
                    join(0, 0, again=False)
                    join(0, 1, again=False)
                    with dve.Fori(1, NG // 2) as i:
                        join(i, 0)
                        join(i, 1)
                    for s in range(2):
                        dve.wait_ge(stored[s], NG // 2 * 16)
            ph.end()

        with Phase("l1u") as ph:
            mean, var, root = (ph.sb(n, [P, D]) for n in ("mean", "var", "root"))
            tot = [ph.sb(f"tot{k}", [P, D]) for k in range(2)]
            p_a = [ph.ps(f"p_a{k}", [P, 512]) for k in range(2)]
            summed, varied, rooted = (ph.sem(n) for n in ("summed", "varied", "rooted"))
            with nc.Block() as block:
                @block.tensor
                def _(pe):
                    for k, t in enumerate((sums, squares)):
                        ins = pe.matmul(p_a[k][:, :], ones[:, :], t[:, :], start=True, stop=True)
                    ins.then_inc(summed, 1)

                @block.scalar
                def _(act):
                    act.wait_ge(varied, 1)
                    act.activation(root[:, :], var[:, :], ACT.Sqrt, bias=eps_t[:, :]).then_inc(rooted, 1)

                @block.vector
                def _(dve):
                    dve.wait_ge(summed, 1)
                    for k in range(2):
                        dve.tensor_reduce(tot[k][:, :], p_a[k][:, :].rearrange("p (t f) -> p f t", f=D), AX, ALU.add)
                    dve.drain()
                    norm_terms(dve, tot[0][:, :], tot[1][:, :], g2r[:, :], be2r[:, :], b2r[:, :], mean[:, :], var[:, :],
                               root[:, :], rooted, scale2[:, :], shift2[:, :], varied)
            ph.end()

        with Phase("l1c") as ph:
            mt = [ph.sb(f"mt{s}", [P, G, SR]) for s in range(2)]
            h = [ph.sb(f"h{s}", [P, GD]) for s in range(2)]
            u = [ph.sb(f"u{s}", [P, GD]) for s in range(2)]
            hit = [ph.sb(f"hit{s}", [P, G, LO]) for s in range(2)]
            p_sum = [ph.ps(f"p_sum{s}", [P, 512]) for s in range(2)]
            in_ = [ph.sem(f"in_{s}") for s in range(2)]
            hits, moved, relued, summed, added, begun = (ph.sem(n) for n in ("hits", "moved", "relued", "summed", "added", "begun"))
            with nc.Block() as block:
                @block.sync
                def _(sp):
                    with sp.Fori(0, NG // 2) as i:
                        for s in range(2):
                            g = i * 2 + s
                            sp.wait_ge(summed, g + 1)
                            sp.sem_inc(begun, 1)
                            sp.dma_start(h[s][:, :], edge_h2[:, bass.ds(g * GD, GD)]).then_inc(in_[s], 16)
                            sp.dma_start(mt[s][:, :, :], by_src[:, bass.ds(g * G, G), :]).then_inc(in_[s], 16)

                @block.scalar
                def _(act):
                    with act.Fori(0, NG // 2) as i:
                        for s in range(2):
                            act.wait_ge(moved, i * 2 + (s + 1))
                            act.activation(u[s][:, :], u[s][:, :], ACT.Relu).then_inc(relued, 1)

                @block.vector
                def _(dve):
                    def group(i, s, again=True):
                        g = (i - 1) * 2 + s
                        if again:
                            dve.load(add_regs, off_s[0:1, bass.ds(g * G, G)])
                        dve.wait_ge(in_[s], i * 32 + 32)
                        dve.wait_ge(summed, i * 2 + (s + 1))
                        v = u[s][:, :].rearrange("p (t f) -> p t f", f=D)
                        wide = [P, G, D]
                        dve.tensor_tensor(v, h[s][:, :].rearrange("p (t f) -> p t f", f=D),
                                          scale2[:, None, :].broadcast_to(wide), ALU.mult)
                        for j in range(G):
                            if j == 4:
                                dve.drain()
                                dve.tensor_tensor(v, v, shift2[:, None, :].broadcast_to(wide), ALU.add).then_inc(moved, 1)
                            ins = dve.tensor_scalar(hit[s][:, j, :], iota_lo[:, :], mt[s][:, j, 1:2], None, ALU.is_equal)
                            if j == G - 1:
                                ins.then_inc(hits, 1)
                            if again:
                                add(g, s, j)

                    def add(g, s, j):
                        at = dve.snap(add_regs[j], min_val=0, max_val=W - D)
                        to = ACC[0:LO, bass.ds(at, D)]
                        if j == 0:
                            dve.wait_ge(summed, g + 3)
                        dve.wait_ge(added, g * G + (j + AHEAD))
                        dve.tensor_tensor(to, to, p_sum[s][0:LO, j * D:(j + 1) * D], ALU.add).then_inc(added, 1)

                    dve.sem_inc(added, AHEAD)
                    group(0, 0, again=False)
                    group(0, 1, again=False)
                    with dve.Fori(1, NG // 2) as i:
                        group(i, 0)
                        group(i, 1)
                    add_sums(dve, added, summed, p_sum, off_s, ACC, NG - 2, 0)
                    add_sums(dve, added, summed, p_sum, off_s, ACC, NG - 1, 1)

                @block.tensor
                def _(pe):
                    pe.sem_inc(summed, 2)
                    with pe.Fori(0, NG // 2) as i:
                        for s in range(2):
                            pe.wait_ge(hits, i * 2 + (s + 1))
                            pe.wait_ge(relued, i * 2 + (s + 1))
                            pe.wait_ge(added, (i * 2 + s) * G + G)
                            for j in range(G):
                                ins = pe.matmul(p_sum[s][0:LO, j * D:(j + 1) * D], hit[s][:, j, :],
                                                u[s][:, j * D:(j + 1) * D], start=True, stop=True)
                            ins.then_inc(summed, 1)
            ph.end()

        def residual(tag, y):
            with nc.Block() as block:
                @block.vector
                def _(dve):
                    dve.tensor_tensor(TMP[:, :], X[:, :], y[:, :], ALU.add)
                    dve.drain()
                    dve.memset(ACC[:, :], 0.0)
            layer_norm(tag, TMP, X)

        residual("l1n", ACC)
        inv_root, inv_deg = sb("inv_root", [LO, NB]), sb("inv_deg", [LO, NB])

        with Phase("l2d") as ph:
            root, one_more, rooted = ph.sb("root", [LO, NB]), ph.sem("one_more"), ph.sem("rooted")
            with nc.Block() as block:
                @block.vector
                def _(dve):
                    dve.tensor_scalar(deg[:, :], deg[:, :], 1.0, None, ALU.add).then_inc(one_more, 1)
                    dve.wait_ge(one_more, 1)
                    dve.reciprocal(inv_deg[:, :], deg[:, :])
                    dve.wait_ge(rooted, 1)
                    dve.reciprocal(inv_root[:, :], root[:, :])
                    dve.drain()
                    dve.tensor_tensor(f3(TMP), f3(X), per_bucket(inv_root), ALU.mult)

                @block.scalar
                def _(act):
                    act.wait_ge(one_more, 1)
                    act.activation(root[:, :], deg[:, :], ACT.Sqrt).then_inc(rooted, 1)
            ph.end()

        def gcn_sum(tag, v):
            with Phase(tag) as ph:
                own = ph.sb("own", [LO, W])
                with nc.Block() as block:
                    @block.vector
                    def _(dve):
                        dve.tensor_tensor(f3(ACC), f3(ACC), per_bucket(inv_root), ALU.mult)
                        dve.tensor_tensor(f3(own), f3(v), per_bucket(inv_deg), ALU.mult)
                        dve.drain()
                        dve.tensor_tensor(ACC[:, :], ACC[:, :], own[:, :], ALU.add)
                ph.end()

        store_table("l2t", [(nodes(table), f3(TMP))])
        gather_sum("l2a", dst_meta, 2, table, False, off_d, ACC)
        gcn_sum("l2e", X)

        V = sb("V", [LO, W])
        with Phase("l2w") as ph:
            turned = [ph.sb(f"turned{s}", [P, LO]) for s in range(2)]
            hid = [ph.sb(f"hid{s}", [P, 2 * LO]) for s in range(2)]
            p_t = [ph.ps(f"p_t{s}", [P, 512]) for s in range(2)]
            p_c = [ph.ps(f"p_c{s}", [P, 512]) for s in range(2)]
            p_o = [ph.ps(f"p_o{s}", [P, 512]) for s in range(2)]
            t_ok, c_ok, m_ok, h_ok, o_ok, taken = (ph.sem(n) for n in ("t_ok", "c_ok", "m_ok", "h_ok", "o_ok", "taken"))
            with nc.Block() as block:
                @block.tensor
                def _(pe):
                    for n in range(Q + 2):
                        if n < Q:
                            if n >= 2:
                                pe.wait_ge(c_ok, n - 1)
                            pe.transpose(p_t[n % 2][:, 0:LO], ACC[:, n * P:(n + 1) * P], ident[0:LO, 0:LO]).then_inc(t_ok, 1)
                        if 1 <= n <= Q:
                            q = n - 1
                            pe.wait_ge(c_ok, q + 1)
                            if q >= 2:
                                pe.wait_ge(h_ok, q - 1)
                            for k in range(2):
                                ins = pe.matmul(p_c[q % 2][:, k * LO:(k + 1) * LO], w21[k][:, :], turned[q % 2][:, :],
                                                start=True, stop=True)
                            ins.then_inc(m_ok, 1)
                        if n >= 2:
                            q = n - 2
                            pe.wait_ge(h_ok, q + 1)
                            if q >= 2:
                                pe.wait_ge(taken, q - 1)
                            for k in range(2):
                                ins = pe.matmul(p_o[q % 2][0:LO, k * 2 * D:(k + 1) * 2 * D],
                                                hid[q % 2][:, k * LO:(k + 1) * LO], w22[:, :], start=True, stop=True)
                            ins.then_inc(o_ok, 1)

                @block.scalar
                def _(act):
                    for n in range(Q + 1):
                        if n < Q:
                            act.wait_ge(t_ok, n + 1)
                            if n >= 2:
                                act.wait_ge(m_ok, n - 1)
                            act.copy(turned[n % 2][:, :], p_t[n % 2][:, 0:LO]).then_inc(c_ok, 1)
                        if n >= 1:
                            q = n - 1
                            act.wait_ge(m_ok, q + 1)
                            if q >= 2:
                                act.wait_ge(o_ok, q - 1)
                            act.activation(hid[q % 2][:, :], p_c[q % 2][:, 0:2 * LO], ACT.Identity,
                                           bias=b21c[:, :]).then_inc(h_ok, 1)

                @block.vector
                def _(dve):
                    for q in range(Q):
                        dve.wait_ge(o_ok, q + 1)
                        dve.tensor_copy(V[:, q * P:(q + 1) * P], p_o[q % 2][0:LO, 0:P]).then_inc(taken, 1)
                    dve.wait_ge(taken, Q)
                    dve.tensor_tensor(f3(TMP), f3(V), per_bucket(inv_root), ALU.mult)
                    dve.wait_ge(m_ok, Q)
                    dve.memset(ACC[:, :], 0.0)
            ph.end()

        store_table("l2u", [(nodes(table), f3(TMP))])
        gather_sum("l2b", dst_meta, 2, table, False, off_d, ACC)
        gcn_sum("l2f", V)
        with nc.Block() as block:
            @block.vector
            def _(dve):
                dve.tensor_tensor(f3(V), f3(ACC), b22r[0:LO, None, :].broadcast_to([LO, NB, D]), ALU.add)
                dve.drain()
                dve.tensor_scalar(V[:, :], V[:, :], 0.0, None, ALU.max)
        residual("l2n", V)
        STATE = sb("STATE", [LO, NB, 2 * D])
        SUMS = STATE[:, :, :].rearrange("l b f -> l (b f)")
        off_d2 = sb("off_d2", [1, TILES], I32)
        state_t = sb("state_t", [P, Q * LO])

        def first_state(dve, q, p):
            return dve.tensor_tensor(f3(V)[:, 4 * q:4 * q + 4, :], p[0].rearrange("l (b f) -> l b f", f=D),
                                     lin0b[0:LO, None, :].broadcast_to([LO, 4, D]), ALU.add)

        node_products("l3i", X, [lin0], first_state)
        with nc.Block() as block:
            @block.vector
            def _(dve):
                dve.tensor_scalar(V[:, :], V[:, :], 0.0, None, ALU.max)
                dve.tensor_scalar(off_d2[:, :], off_d[:, :], 2.0, None, ALU.mult)

        class StateProducts:

            def __init__(self, ph):
                self.p_t = ph.ps("sp_t", [P, 512])
                self.p_b = ph.ps("sp_b", [P, 512])
                self.t_ok, self.c_ok, self.b_ok, self.taken, self.stored = (
                    ph.sem(n) for n in ("st_ok", "sc_ok", "sb_ok", "staken", "sstored"))

            def turn(self, pe, q):
                if q >= 1:
                    pe.wait_ge(self.c_ok, q)
                pe.transpose(self.p_t[:, 0:LO], V[:, q * P:(q + 1) * P], ident[0:LO, 0:LO]).then_inc(self.t_ok, 1)

            def copy(self, act, q):
                act.wait_ge(self.t_ok, q + 1)
                act.copy(STATE[:, 4 * q:4 * q + 4, 0:D], f3(V)[:, 4 * q:4 * q + 4, :])
                act.copy(state_t[:, q * LO:(q + 1) * LO], self.p_t[:, 0:LO]).then_inc(self.c_ok, 1)

            def times(self, pe, q):
                pe.wait_ge(self.c_ok, q + 1)
                if q >= 1:
                    pe.wait_ge(self.taken, q)
                pe.matmul(self.p_b[0:LO, 0:P], state_t[:, q * LO:(q + 1) * LO], en2b[:, :],
                          start=True, stop=True).then_inc(self.b_ok, 1)

            def take(self, dve, q):
                dve.wait_ge(self.b_ok, q + 1)
                dve.tensor_copy(STATE[:, 4 * q:4 * q + 4, D:2 * D],
                                self.p_b[0:LO, 0:P].rearrange("l (b f) -> l b f", f=D)).then_inc(self.taken, 1)

            def store(self, sp):
                rows = wide_table[0:N, :].rearrange("(l b) f -> l b f", b=NB)
                for q in range(Q):
                    sp.wait_ge(self.taken, q + 1)
                    sp.dma_start(rows[:, 4 * q:4 * q + 4, :], STATE[:, 4 * q:4 * q + 4, :]).then_inc(self.stored, 16)
                sp.wait_ge(self.stored, 16 * Q)

        with Phase("l3s") as ph:
            products = StateProducts(ph)
            with nc.Block() as block:
                @block.sync
                def _(sp):
                    products.store(sp)

                @block.tensor
                def _(pe):
                    products.turn(pe, 0)
                    for q in range(Q):
                        if q + 1 < Q:
                            products.turn(pe, q + 1)
                        products.times(pe, q)

                @block.scalar
                def _(act):
                    for q in range(Q):
                        products.copy(act, q)

                @block.vector
                def _(dve):
                    for q in range(Q):
                        products.take(dve, q)
            ph.end()
        with nc.Fori(0, STEPS) as step:
            with Phase("l3m") as ph:
                HD = D * D
                OWN = 20 * D
                REST = HD - OWN
                RING = 4
                mt = [ph.sb(f"mt{s}", [P, G, 2]) for s in range(2)]
                hid = [ph.sb(f"hid{s}", [P, G * P]) for s in range(2)]
                xg = [ph.sb(f"xg{s}", [P, G, 3 * D]) for s in range(2)]
                apart = [ph.sb(f"apart{s}", [P, G, LO]) for s in range(2)]
                prod = [ph.sb(f"prod{r}", [P, HD]) for r in range(RING)]
                rest = [ph.sb(f"rest{r}", [P, REST]) for r in range(RING)]
                p_w = [ph.ps(f"p_w{s}", [P, HD]) for s in range(2)]
                p_sum = [ph.ps(f"p_sum{s}", [P, G * 2 * D]) for s in range(2)]
                meta_in = [ph.sem(f"meta_in{s}") for s in range(2)]
                hid_in = [ph.sem(f"hid_in{s}") for s in range(2)]
                rows_in = [ph.sem(f"rows_in{s}") for s in range(2)]
                distances, hits, mats, used, copied, pooled, msgs, summed, added, begun = (ph.sem(n) for n in (
                    "distances", "hits", "mats", "used", "copied", "pooled", "msgs", "summed", "added", "begun"))
                LATE, LATER = 2, 4
                EARLY = 4
                MATS, USED, POOLED, MSGS, SUMMED, ADDED = 2 * G, 2, RING, RING, 2 * G, 2 * G

                def o_i(t):
                    return t.rearrange("p (o i) -> p o i", i=D)

                def state_of(s, j, n):
                    return xg[s][:, j, None, 0:D].broadcast_to([P, n // D, D])

                with nc.Block() as block:
                    @block.sync
                    def _(sp):
                        with sp.Fori(0, NG // 2) as i:
                            for s in range(2):
                                g = i * 2 + s
                                sp.wait_ge(summed, g * G + 1)
                                sp.sem_inc(begun, 1)
                                sp.dma_start(mt[s][:, :, :], dst_meta[:, bass.ds(g * G, G), :]).then_inc(meta_in[s], 16)
                                sp.wait_ge(mats, g * G + G)
                                sp.sem_inc(begun, 1)
                                sp.dma_start(hid[s][:, :], hid_t[:, bass.ds(g * (G * P), G * P)]).then_inc(hid_in[s], 16)

                    @block.gpsimd
                    def _(pool):
                        def gather(i, s, j):
                            g = i * 2 + s
                            if j == 0:
                                pool.wait_ge(meta_in[s], i * 16 + 16)
                            pool.wait_ge(summed, g * G + (j + 1))
                            pool.sem_inc(begun, 1)
                            pool.indirect_dma_start(
                                xg[s][:, j, 0:2 * D], None, wide_table[:, :],
                                bass.IndirectOffsetOnAxis(ap=mt[s][:, j, 0:1].bitcast(I32), axis=0)).then_inc(rows_in[s], 16)

                        def times(i, s, j):
                            t = (i * 2 + s) * G + j
                            pool.wait_ge(copied, t + 1)
                            pool.wait_ge(msgs, t + 1)
                            pool.tensor_tensor(o_i(prod[j % RING][:, OWN:HD]), o_i(rest[j % RING][:, :]),
                                               state_of(s, j, REST), ALU.mult).then_inc(pooled, 1)

                        def group(i, s, left=2):
                            pool.wait_ge(rows_in[s], i * (16 * G) + 16 * G)
                            for j in range(G):
                                times(i, s, j)
                                if j + EARLY < G:
                                    if left >= 1:
                                        gather(i + s, 1 - s, j + EARLY)
                                elif left >= 2:
                                    gather(i + 1, s, j + EARLY - G)

                        pool.sem_inc(pooled, POOLED)
                        for j in range(G):
                            gather(0, 0, j)
                        for j in range(EARLY):
                            gather(0, 1, j)
                        with pool.Fori(0, NG // 2 - 1) as i:
                            group(i, 0)
                            group(i, 1)
                        group(NG // 2 - 1, 0, left=1)
                        group(NG // 2 - 1, 1, left=0)

                    @block.scalar
                    def _(act):
                        def distance(i, s, j):
                            g = i * 2 + s
                            if j == 0:
                                act.wait_ge(meta_in[s], i * 16 + 16)
                            act.wait_ge(summed, g * G + (j + 1))
                            act.activation(apart[s][:, j, :], iota_lo[:, :], ACT.Abs, scale=-1.0,
                                           bias=mt[s][:, j, 1:2]).then_inc(distances, 1)
                            if j % 4 == 3:
                                act.wait_ge(distances, g * G + (j + 1))
                                quarter = apart[s][:, j - 3:j + 1, :]
                                act.activation(quarter, quarter, ACT.Relu, scale=-1.0, bias=ones[:, 0:1]).then_inc(hits, 1)

                        def copy(i, s, j):
                            t = (i * 2 + s) * G + j
                            act.wait_ge(mats, t + (MATS + 1))
                            act.wait_ge(pooled, t + 1)
                            act.copy(rest[j % RING][:, :], p_w[j % 2][:, OWN:HD]).then_inc(copied, 1)

                        def group(i, s, last=False):
                            for j in range(G):
                                copy(i, s, j)
                                if not last:
                                    distance(i + s, 1 - s, j)

                        for j in range(G):
                            distance(0, 0, j)
                        with act.Fori(0, NG // 2 - 1) as i:
                            group(i, 0)
                            group(i, 1)
                        group(NG // 2 - 1, 0)
                        group(NG // 2 - 1, 1, last=True)

                    @block.tensor
                    def _(pe):
                        def matrices(i, s, j):
                            t = (i * 2 + s) * G + j
                            pe.wait_ge(used, t + 1)
                            for c in range(2):
                                ins = pe.matmul(p_w[j % 2][:, c * 512:(c + 1) * 512], hid[s][:, j * P:(j + 1) * P],
                                                en2[:, c * 512:(c + 1) * 512], start=True, stop=True)
                            ins.then_inc(mats, 1)

                        def sum_up(i, s, j):
                            g = i * 2 + s
                            if j == 0:
                                pe.wait_ge(hits, g * 4 + 4)
                                pe.wait_ge(rows_in[s], i * (16 * G) + 16 * G)
                                pe.wait_ge(added, g * G + G)
                            pe.wait_ge(msgs, g * G + (j + 1 + MSGS))
                            pe.matmul(p_sum[s][0:LO, j * 2 * D:(j + 1) * 2 * D], apart[s][:, j, :],
                                      xg[s][:, j, D:3 * D], start=True, stop=True).then_inc(summed, 1)

                        def group(i, s, first=False):
                            pe.wait_ge(hid_in[s], i * 16 + 16)
                            for j in range(G):
                                matrices(i, s, j)
                                if j >= LATER:
                                    sum_up(i, s, j - LATER)
                                elif not first:
                                    sum_up(i + (s - 1), 1 - s, G - LATER + j)

                        pe.sem_inc(summed, SUMMED)
                        pe.sem_inc(mats, MATS)
                        group(0, 0, first=True)
                        group(0, 1)
                        with pe.Fori(1, NG // 2) as i:
                            group(i, 0)
                            group(i, 1)
                        for j in range(G - LATER, G):
                            sum_up(NG // 2 - 1, 1, j)

                    @block.vector
                    def _(dve):
                        def add(g, s, j):
                            at = dve.snap(add_regs[j], min_val=0, max_val=2 * (W - D))
                            to = SUMS[0:LO, bass.ds(at, 2 * D)]
                            if j % (G // 2) == 0:
                                dve.wait_ge(summed, g * G + (j + G // 2 + SUMMED))
                            dve.wait_ge(added, g * G + (j + ADDED))
                            dve.tensor_tensor(to, to, p_sum[s][0:LO, j * 2 * D:(j + 1) * 2 * D],
                                              ALU.add).then_inc(added, 1)

                        def reduce(g, s, j):
                            t = g * G + j
                            dve.wait_ge(used, t + (USED + 1))
                            dve.wait_ge(pooled, t + (POOLED + 1))
                            dve.tensor_reduce(xg[s][:, j, 2 * D:3 * D], o_i(prod[j % RING][:, :]), AX,
                                              ALU.add).then_inc(msgs, 1)

                        def group(i, s, first=False):
                            g = i * 2 + s
                            if not first:
                                dve.load(add_regs, off_d2[0:1, bass.ds((g - 1) * G, G)])
                            dve.wait_ge(rows_in[s], i * (16 * G) + 16 * G)
                            for j in range(G):
                                dve.wait_ge(mats, g * G + (j + 1 + MATS))
                                dve.wait_ge(msgs, g * G + (j + 1))
                                dve.tensor_tensor(o_i(prod[j % RING][:, 0:512]), o_i(p_w[j % 2][:, 0:512]),
                                                  state_of(s, j, 512), ALU.mult)
                                dve.wait_ge(copied, g * G + (j + 1))
                                dve.tensor_tensor(o_i(prod[j % RING][:, 512:OWN]), o_i(p_w[j % 2][:, 512:OWN]),
                                                  state_of(s, j, OWN - 512), ALU.mult).then_inc(used, 1)
                                if not first:
                                    add(g - 1, 1 - s, j)
                                if j >= LATE:
                                    reduce(g, s, j - LATE)
                                elif not first:
                                    reduce(g - 1, 1 - s, G - LATE + j)

                        dve.memset(SUMS[:, :], 0.0)
                        dve.drain().then_inc(used, USED)
                        dve.sem_inc(msgs, MSGS)
                        dve.sem_inc(added, ADDED)
                        group(0, 0, first=True)
                        group(0, 1)
                        with dve.Fori(1, NG // 2) as i:
                            group(i, 0)
                            group(i, 1)
                        for j in range(G - LATE, G):
                            reduce(NG - 1, 1, j)
                        dve.load(add_regs, off_d2[0:1, bass.ds((NG - 1) * G, G)])
                        for j in range(G):
                            add(NG - 1, 1, j)
                ph.end()

            with Phase("l3g") as ph:
                products = StateProducts(ph)
                m_t = [ph.sb(f"m_t{s}", [P, LO]) for s in range(2)]
                gate = [ph.sb(f"gate{s}", [LO, 2 * P]) for s in range(2)]
                new = [ph.sb(f"new{s}", [LO, 4, D]) for s in range(2)]
                diff = [ph.sb(f"diff{s}", [LO, 4, D]) for s in range(2)]
                p_t = [ph.ps(f"p_t{s}", [P, 512]) for s in range(2)]
                p_g = [ph.ps(f"p_g{s}", [P, 512]) for s in range(2)]
                t_ok, m_ok, g_ok, s_ok, n_in, n_ok, h_ok, joined = (ph.sem(n) for n in (
                    "t_ok", "m_ok", "g_ok", "s_ok", "n_in", "n_ok", "h_ok", "joined"))

                def part(q, k):
                    return p_g[q % 2][0:LO, k * P:(k + 1) * P].rearrange("l (b f) -> l b f", b=4)

                with nc.Block() as block:
                    @block.sync
                    def _(sp):
                        products.store(sp)

                    @block.tensor
                    def _(pe):
                        pe.wait_ge(joined, 1)
                        for n in range(Q + 4):
                            if n < Q:
                                if n >= 2:
                                    pe.wait_ge(m_ok, n - 1)
                                pe.transpose(p_t[n % 2][:, 0:LO], ACC[:, n * P:(n + 1) * P],
                                             ident[0:LO, 0:LO]).then_inc(t_ok, 1)
                            if 1 <= n <= Q:
                                q = n - 1
                                if q >= 2:
                                    pe.wait_ge(n_in, q - 1)
                                to = p_g[q % 2][0:LO, :]
                                pe.matmul(to, ones[0:2, 0:LO], gbias[:, :], start=True, stop=False)
                                h = state_t[:, q * LO:(q + 1) * LO]
                                pe.matmul(to[:, 0:2 * P], h, whh[:, 0:2 * P], start=False, stop=False,
                                          skip_group_check=True)
                                pe.matmul(to[:, 3 * P:4 * P], h, whh[:, 2 * P:3 * P], start=False, stop=False,
                                          skip_group_check=True)
                                pe.wait_ge(m_ok, q + 1)
                                pe.matmul(to, m_t[q % 2][:, :], wih[:, :], start=False, stop=True).then_inc(g_ok, 1)
                            if 3 <= n < Q + 3:
                                pe.wait_ge(h_ok, n - 2)
                                products.turn(pe, n - 3)
                            if n >= 4:
                                products.times(pe, n - 4)

                    @block.scalar
                    def _(act):
                        for n in range(Q + 3):
                            if n < Q:
                                act.wait_ge(t_ok, n + 1)
                                if n >= 2:
                                    act.wait_ge(g_ok, n - 1)
                                act.activation(m_t[n % 2][:, :], p_t[n % 2][:, 0:LO], ACT.Relu,
                                               bias=convb[:, :]).then_inc(m_ok, 1)
                            if 1 <= n <= Q:
                                q = n - 1
                                act.wait_ge(g_ok, q + 1)
                                if q >= 2:
                                    act.wait_ge(h_ok, q - 1)
                                act.activation(gate[q % 2][:, :], p_g[q % 2][0:LO, 0:2 * P], ACT.Sigmoid).then_inc(s_ok, 1)
                            if 2 <= n < Q + 2:
                                q = n - 2
                                act.wait_ge(n_in, q + 1)
                                act.activation(new[q % 2][:, :, :], new[q % 2][:, :, :], ACT.Tanh).then_inc(n_ok, 1)
                            if n >= 3:
                                products.copy(act, n - 3)

                    @block.vector
                    def _(dve):
                        both = SUMS[:, :].rearrange("l (b f) -> l b f", f=2 * D)
                        dve.tensor_tensor(f3(ACC), both[:, :, 0:D], both[:, :, D:2 * D], ALU.add).then_inc(joined, 1)
                        for n in range(1, Q + 4):
                            if n <= Q:
                                q = n - 1
                                dve.wait_ge(s_ok, q + 1)
                                if q >= 2:
                                    dve.wait_ge(h_ok, q - 1)
                                c = new[q % 2][:, :, :]
                                dve.tensor_tensor(c, gate[q % 2][:, 0:P].rearrange("l (b f) -> l b f", b=4), part(q, 3), ALU.mult)
                                dve.drain()
                                dve.tensor_tensor(c, c, part(q, 2), ALU.add).then_inc(n_in, 1)
                            if 2 <= n < Q + 2:
                                q = n - 2
                                state = f3(V)[:, 4 * q:4 * q + 4, :]
                                d = diff[q % 2][:, :, :]
                                dve.wait_ge(n_ok, q + 1)
                                dve.tensor_tensor(d, state, new[q % 2][:, :, :], ALU.subtract)
                                dve.drain()
                                dve.tensor_tensor(d, d, gate[q % 2][:, P:2 * P].rearrange("l (b f) -> l b f", b=4), ALU.mult)
                                dve.drain()
                                dve.tensor_tensor(state, d, new[q % 2][:, :, :], ALU.add).then_inc(h_ok, 1)
                            if n >= 4:
                                products.take(dve, n - 4)
                ph.end()

        with nc.Block() as block:
            @block.vector
            def _(dve):
                dve.tensor_tensor(TMP[:, :], X[:, :], V[:, :], ALU.add)
        layer_norm("l3n", TMP, X)
        store_table("end", [(out.rearrange("(l b) f -> l (b f)", b=NB), X[:, :])])


def arranged(inputs):
    x = {k: np.asarray(v) for k, v in inputs.items()}
    pad = EP - E

    def t(name):
        return np.ascontiguousarray(x[name].T)

    arrays = {
        "x": np.concatenate([x["x"], np.zeros((1, D), np.float32)]),
        "zeros": np.zeros((1, 2 * D), np.float32),
        "src": np.concatenate([x["src"], np.full(pad, N, x["src"].dtype)]),
        "dst": np.concatenate([x["dst"], np.full(pad, N, x["dst"].dtype)]),
        "edge_weight": np.concatenate([x["edge_weight"], np.zeros(pad, np.float32)]),
        "edge_attr_32": np.concatenate([x["edge_attr_32"], np.zeros((pad, D), np.float32)]),
        "lin0_t": t("L3_gnn_lin0_w"),
        "en1_t": t("L3_gnn_en1_w"),
        "wih_t": t("L3_gnn_gru_wih"),
        "whh_t": t("L3_gnn_gru_whh"),
        "en2_t": np.ascontiguousarray(x["L3_gnn_en2_w"].reshape(D, D, EH).transpose(2, 1, 0).reshape(EH, D * D)),
        "en2_b": x["L3_gnn_en2_b"].reshape(D, D),
    }
    for name in ("L0_gnn_weight", "L1_gnn_W1", "L1_gnn_b1", "L1_gnn_gamma1", "L1_gnn_beta1", "L1_gnn_W2",
                 "L1_gnn_b2", "L1_gnn_gamma2", "L1_gnn_beta2", "L2_gnn_W1", "L2_gnn_b1", "L2_gnn_W2", "L2_gnn_b2",
                 "L3_gnn_lin0_b", "L3_gnn_en1_b", "L3_gnn_conv_bias", "L3_gnn_gru_bih", "L3_gnn_gru_bhh"):
        arrays[name] = x[name]
    return arrays


def kernel(**inputs):
    import concourse.bacc as bacc
    from concourse.bass_utils import run_bass_kernel_spmd

    nc = bacc.Bacc("TRN2", target_bir_lowering=False, num_devices=1)
    arrays, args = {}, {}
    for name, v in arranged(inputs).items():
        arrays[f"in_{name}"] = np.ascontiguousarray(v)
        args[name] = nc.dram_tensor(f"in_{name}", v.shape, mybir.dt.from_np(v.dtype), kind="ExternalInput").ap()
    out = nc.dram_tensor("out_x", (N, D), F32, kind="ExternalOutput").ap()
    build(nc, args, out)
    r = run_bass_kernel_spmd(nc, [arrays], core_ids=[0])
    return r.results[0]["out_x"]
```
